# Optimizing a Trainium2 kernel written in Bass

```python
import numpy as np
import jax
import jax.numpy as jnp

def _softmax(x, axis=-1):
    return jax.nn.softmax(x, axis=axis)

def _gelu(x):
    return jax.nn.gelu(x, approximate=True)

def _silu(x):
    return jax.nn.silu(x)

def _sigmoid(x):
    return jax.nn.sigmoid(x)

def _layernorm(x, axis=-1, eps=1e-05):
    m = jnp.mean(x, axis=axis, keepdims=True)
    v = jnp.var(x, axis=axis, keepdims=True)
    return (x - m) / jnp.sqrt(v + eps)

def _scatter_add(tgt, idx, src, axis=0):
    return tgt.at[idx].add(src)

def _segment_sum(src, seg, n):
    return jax.ops.segment_sum(src, seg, n)
kernel_name = 'mk_adj_resnorm_d1_adj_r2_0924a8'

def setup_inputs(seed: int=0):
    np.random.seed(seed)
    _w = jnp.asarray

    def _rec_inputs():
        import jax
        import jax.numpy as jnp
        _gk = jax.random.key(seed)
        x = 7.22e-05 + 1 * jax.random.normal(jax.random.fold_in(_gk, 1), (64, 128, 512), jnp.float32)
        _w = (1.0 + jnp.arange(128, dtype=jnp.float32)) ** (-0.5)
        _w = _w / _w.mean()
        _pij = jnp.clip(0.125 * _w[:, None] * _w[None, :], 0.0, 1.0)
        _a = jax.random.uniform(jax.random.fold_in(_gk, 2), (64, 128, 128)) < _pij
        _a = jnp.logical_or(_a, jnp.eye(128, dtype=bool))
        adj = _a.astype(jnp.int32)
        return (x, adj)
    x, adj = _rec_inputs()

    def _L0_gnn_setup():
        import jax, jax.numpy as jnp
        import numpy as np
        import math
        D_MODEL = 512
        N_HEADS = 16
        D_HEAD = D_MODEL // N_HEADS
        B, S = (4, 1024)
        key = jax.random.key(seed)
        ks = jax.random.split(key, 10)
        x = jax.random.normal(ks[0], (B, S, D_MODEL), dtype=jnp.float32)
        mask = jax.random.randint(ks[1], (B, S, S), 0, 2, dtype=jnp.int32)
        eye = jnp.eye(S, dtype=jnp.int32)[None]
        mask = jnp.maximum(mask, eye)
        std = 1.0 / math.sqrt(D_MODEL)
        Wq = jax.random.normal(ks[2], (D_MODEL, D_MODEL), dtype=jnp.float32) * std
        Wk = jax.random.normal(ks[3], (D_MODEL, D_MODEL), dtype=jnp.float32) * std
        Wv = jax.random.normal(ks[4], (D_MODEL, D_MODEL), dtype=jnp.float32) * std
        Wo = jax.random.normal(ks[5], (D_MODEL, D_MODEL), dtype=jnp.float32) * std
        bq = jnp.zeros((D_MODEL,), dtype=jnp.float32)
        bk = jnp.zeros((D_MODEL,), dtype=jnp.float32)
        bv = jnp.zeros((D_MODEL,), dtype=jnp.float32)
        bo = jnp.zeros((D_MODEL,), dtype=jnp.float32)
        return {'x': x, 'mask': mask, 'Wq': Wq, 'bq': bq, 'Wk': Wk, 'bk': bk, 'Wv': Wv, 'bv': bv, 'Wo': Wo, 'bo': bo}
    _L0_gnn_all = _L0_gnn_setup()
    _L0_gnn_in = {k: v for k, v in _L0_gnn_all.items() if k in ('Wq', 'bq', 'Wk', 'bk', 'Wv', 'bv', 'Wo', 'bo')}
    del _L0_gnn_all
    return {'x': x, 'adj': adj, 'L0_gnn_Wq': _L0_gnn_in['Wq'], 'L0_gnn_bq': _L0_gnn_in['bq'], 'L0_gnn_Wk': _L0_gnn_in['Wk'], 'L0_gnn_bk': _L0_gnn_in['bk'], 'L0_gnn_Wv': _L0_gnn_in['Wv'], 'L0_gnn_bv': _L0_gnn_in['bv'], 'L0_gnn_Wo': _L0_gnn_in['Wo'], 'L0_gnn_bo': _L0_gnn_in['bo']}

def reference(x, adj, L0_gnn_Wq, L0_gnn_bq, L0_gnn_Wk, L0_gnn_bk, L0_gnn_Wv, L0_gnn_bv, L0_gnn_Wo, L0_gnn_bo):
    import jax
    import jax.numpy as jnp

    def _L0_gnn_ref(x, mask, Wq, bq, Wk, bk, Wv, bv, Wo, bo):
        import jax, jax.numpy as jnp
        import numpy as np
        import math
        D_MODEL = 512
        N_HEADS = 16
        D_HEAD = D_MODEL // N_HEADS
        B, S = (4, 1024)
        b, s, _ = x.shape
        scale = 1.0 / math.sqrt(D_HEAD)

        def heads(t):
            return t.reshape(b, s, N_HEADS, D_HEAD).transpose(0, 2, 1, 3)
        q = heads(x @ Wq + bq)
        k = heads(x @ Wk + bk)
        v = heads(x @ Wv + bv)
        scores = jnp.einsum('bhqd,bhkd->bhqk', q, k) * scale
        scores = jnp.where(mask[:, None] == 0, -jnp.inf, scores)
        attn = jax.nn.softmax(scores, axis=-1)
        out = jnp.einsum('bhqk,bhkd->bhqd', attn, v)
        out = out.transpose(0, 2, 1, 3).reshape(b, s, D_MODEL)
        return out @ Wo + bo
    x = _layernorm(x + _L0_gnn_ref(x, adj, L0_gnn_Wq, L0_gnn_bq, L0_gnn_Wk, L0_gnn_bk, L0_gnn_Wv, L0_gnn_bv, L0_gnn_Wo, L0_gnn_bo), axis=-1)
    return x

_drawn_inputs = setup_inputs


def setup_inputs(seed=0):
    import zlib

    import numpy as np

    out = dict(_drawn_inputs(seed))
    spreads = {'L0_gnn_bq': (0.0, 0.271),
     'L0_gnn_bk': (0.0, 0.8),
     'L0_gnn_bv': (0.0, 0.1),
     'L0_gnn_bo': (0.0, 0.1)}
    factors = {}
    for name, (base, spread) in spreads.items():
        noise = np.random.default_rng([zlib.crc32(name.encode()), seed]).standard_normal(out[name].shape)
        drawn = base * np.exp(spread * noise) if base else spread * noise
        out[name] = jnp.asarray(drawn.astype(out[name].dtype))
    for name, factor in factors.items():
        out[name] = (out[name] * factor).astype(out[name].dtype)
    return out
```

```python
import math
from contextlib import ExitStack

import concourse.bass as bass
from concourse import mybir

F32 = mybir.dt.float32
F32R = mybir.dt.float32r
F16 = mybir.dt.float16
I32 = mybir.dt.int32
ALU = mybir.AluOpType
ACT = mybir.ActivationFunctionType

P = 128
HEADS = 16
UP = 16.0
P_UP = 10
MASKED = -1e30
EPS = 1e-5
GB = 2
QUAD = 32


def build_program(nc, x, adj, Wq, bq, Wk, bk, Wv, bv, Wo, bo, out):
    B, S, D = x.shape
    DH = D // HEADS
    KC = D // P
    HC = HEADS // KC
    NG = B // GB
    SLOTS = GB * KC
    TOK = GB * S
    VC = DH + 1
    VS = DH + 2
    assert S == P and DH == QUAD and KC == 4 and GB == 2 and NG % 2 == 0 and NG >= 6
    EXP_SCALE = 1.0 / (UP * UP * math.sqrt(DH))
    EXP_SHIFT = P_UP * math.log(2.0)
    LAST = NG - 1

    Q, K, V, Y = "q", "k", "v", "y"
    TASKS = {0: (Q, 0), 1: (Q, 1), 2: (K, 0), 3: (K, 1), 4: (Y, 1), 5: (V, 0), 6: (Y, 0), 7: (V, 1), 8: (Y, 1)}
    SPLIT_RANK = {0: 0, 1: 1, 2: 2, 3: 3, 5: 4, 7: 5}
    N_SPLIT = len(SPLIT_RANK)

    def unit(g, s):
        return g * SLOTS + s

    def bank_no(g, s):
        if isinstance(g, int) and g == -1:
            return SPLIT_RANK[s]
        if isinstance(g, int) and g == 0:
            return N_SPLIT + s - (1 if s > 4 else 0)
        if isinstance(g, int) and g == LAST:
            return bank_no(LAST - 1, SLOTS - 1) + {4: 1, 6: 2, 8: 3}[s]
        return g * SLOTS + N_SPLIT - 1 + s

    def bank_of(g, s):
        return (bank_no(g, s) if isinstance(g, int) else N_SPLIT - 1 + s) % 2

    def split_no(g, s):
        return (g + 1) * N_SPLIT + SPLIT_RANK[s]

    def xo_no(g, s):
        if isinstance(g, int) and g >= LAST:
            return 4 * LAST + 3 + {1: 0, 5: 1, 9: 2}[s] - 2
        return g * 4 + 3 + {1: 0, 5: 1, 6: 2, 7: 3}[s]

    def batch(g, b):
        return g * GB + b

    def dma_round(g, k):
        return (g // 2 if isinstance(g, int) else k) + 1

    def wait(eng, sem, value):
        if not isinstance(value, int) or value > 0:
            eng.wait_ge(sem, value)

    def has_next(g):
        return not isinstance(g, int) or g < LAST

    def has_x_next2(g):
        return not isinstance(g, int) or g < LAST - 1

    def all_groups(eng, group):
        group(0, 0, 0)
        group(1, 1, 0)
        with eng.Fori(1, NG // 2 - 1) as k:
            group(2 * k, 0, k)
            group(2 * k + 1, 1, k)
        group(NG - 2, 0, NG // 2 - 1)
        group(NG - 1, 1, NG // 2 - 1)

    with ExitStack() as ctx:
        def sb(name, shape, dt):
            return ctx.enter_context(nc.sbuf_tensor(name, shape, dt))

        def ps(name, shape, dt):
            return ctx.enter_context(nc.psum_tensor(name, shape, dt))

        def sem(name):
            return ctx.enter_context(nc.semaphore(name))

        w_raw = sb("w_raw", [P, 2, KC, D], F32)
        w_hi = {n: sb(f"w{n}_hi", [P, KC, D], F32R) for n in "qkvo"}
        w_lo = {n: sb(f"w{n}_lo", [P, KC, D], F32R) for n in "qkvo"}
        b_qk = sb("b_qk", [P, 2, KC], F32)
        b_qk_up = sb("b_qk_up", [P, 2, KC], F32)
        b_v = sb("b_v", [P, KC], F32)
        b_v_wide = sb("b_v_wide", [P, KC, P], F32)
        b_out = sb("b_out", [P, D], F32)
        ident = sb("ident", [P, P], F32)
        minus_half = sb("minus_half", [P, 1], F32)
        x_in = [sb(f"x_in{i}", [P, GB, D], F32) for i in range(2)]
        x_res = [sb(f"x_res{i}", [P, GB, D], F32) for i in range(2)]
        adj_in = [sb(f"adj_in{i}", [P, GB, S], I32) for i in range(2)]
        mask = [sb(f"mask{i}", [P, GB, S], F32) for i in range(2)]
        xT_hi = [sb(f"xT_hi{i}", [P, KC, TOK], F32R) for i in range(2)]
        xT_lo = [sb(f"xT_lo{i}", [P, KC, TOK], F32R) for i in range(2)]
        part = {(n, h): sb(f"{n}T_{h}", [P, KC, TOK], F16) for n in "qk" for h in ("hi", "lo")}
        stacks = {n: [sb(f"{n}_stack{i}", [P, HEADS, TOK], F16) for i in range(2)] for n in "qk"}
        v_hi = [sb(f"v_hi{i}", [P, GB, HEADS, VS], F16) for i in range(2)]
        v_lo = [sb(f"v_lo{i}", [P, GB, HEADS, VS], F16) for i in range(2)]
        masked = [sb(f"masked{i}", [P, HC, S], F32) for i in range(2)]
        row_max = [sb(f"row_max{i}", [P, HC], F32) for i in range(2)]
        exp_bias = [sb(f"exp_bias{i}", [P, HC], F32) for i in range(2)]
        probs = [sb(f"probs{i}", [P, HC, S], F32) for i in range(2)]
        pT_hi = [sb(f"pT_hi{i}", [P, HC, S], F16) for i in range(2)]
        pT_lo = [sb(f"pT_lo{i}", [P, HC, S], F16) for i in range(2)]
        inv_sum = [sb(f"inv_sum{i}", [P, HC], F32) for i in range(2)]
        attn = [sb(f"attn{i}", [P, D], F32) for i in range(2)]
        aT_hi = sb("aT_hi", [P, KC, S], F32R)
        aT_lo = sb("aT_lo", [P, KC, S], F32R)
        y = [sb(f"y{i}", [P, D], F32) for i in range(2)]
        stats = [sb(f"stats{i}", [P, 6], F32) for i in range(2)]
        moments = [sb(f"moments{i}", [P, 2], F32) for i in range(2)]
        minus_mean = [sb(f"minus_mean{i}", [P, 1], F32) for i in range(2)]
        var_eps = [sb(f"var_eps{i}", [P, 1], F32) for i in range(2)]
        inv_std = [sb(f"inv_std{i}", [P, 1], F32) for i in range(2)]

        score_ps = [ps(f"score_ps{i}", [P, HC, S], F32) for i in range(2)]
        pT_ps = [ps(f"pT_ps{i}", [P, HC, S], F32) for i in range(2)]
        proj_ps = [ps(f"proj_ps{i}", [P, D], F32) for i in range(2)]
        xo_ps = ps("xo_ps", [P, KC, P], F32)
        av_ps = ps("av_ps", [P, D], F32)
        av_view = av_ps[:, 0:HC * VS].rearrange("p (h c) -> p h c", h=HC)

        x_loaded = [sem(f"x_loaded{i}") for i in range(2)]
        adj_loaded = [sem(f"adj_loaded{i}") for i in range(2)]
        w_loaded = [sem(f"w_loaded{i}") for i in range(4)]
        bias_loaded = sem("bias_loaded")
        spread = {n: [sem(f"{n}_spread{i}") for i in range(2)] for n in "qk"}
        stacked = {n: [sem(f"{n}_stacked{i}") for i in range(2)] for n in "qk"}
        stored = [sem(f"stored{i}") for i in range(2)]
        const_made = sem("const_made")
        ones_made = sem("ones_made")
        w_hi_made = sem("w_hi_made")
        w_lo_made = sem("w_lo_made")
        bias_made = sem("bias_made")
        b_out_mm = sem("b_out_mm")
        b_out_made = sem("b_out_made")
        xo_done = sem("xo_done")
        bank_done = sem("bank_done")
        score_done = sem("score_done")
        pT_done = sem("pT_done")
        av_done = sem("av_done")
        xo_hi = sem("xo_hi")
        split_hi = sem("split_hi")
        exp_done = sem("exp_done")
        pT_hi_done = sem("pT_hi_done")
        xo_out = sem("xo_out")
        bank_out = sem("bank_out")
        mask_made = sem("mask_made")
        max_done = sem("max_done")
        bias_done = sem("bias_done")
        pT_out = sem("pT_out")
        inv_done = sem("inv_done")
        attn_done = sem("attn_done")
        y_done = sem("y_done")
        stats_done = sem("stats_done")
        moments_done = sem("moments_done")
        res_made = sem("res_made")
        ln_small = sem("ln_small")
        ln_done = sem("ln_done")
        vector_goes = sem("vector_goes")
        gpsimd_goes = sem("gpsimd_goes")

        x_dram = x.rearrange("(g b) s d -> g s b d", b=GB)
        adj_dram = adj.rearrange("(g b) s t -> g s b t", b=GB)


        block = ctx.enter_context(nc.Block())

        @block.sync
        def _(sp):
            def load_x(g, par):
                sp.dma_start(x_in[par][:], x_dram[g]).then_inc(x_loaded[par], 16)

            def load_adj(g, par):
                sp.dma_start(adj_in[par][:], adj_dram[g]).then_inc(adj_loaded[par], 16)

            def load_w(i, w):
                sp.dma_start(w_raw[:, i % 2], w.rearrange("(c p) n -> p c n", p=P)).then_inc(w_loaded[i], 16)

            def stack(n, g, par, k):
                sp.wait_ge(bank_out, bank_no(g - 1, 1 if n == "q" else 3) + 1)
                if not isinstance(g, int) or g >= 2:
                    sp.wait_ge(score_done, unit(g - 1, 0))
                t = stacks[n][par]
                heads = t[:].rearrange("p (c j) t -> p c j t", j=HC)
                for j in range(HC):
                    rows = slice(QUAD * j, QUAD * (j + 1))
                    for quad, h in ((0, "hi"), (1 if n == "q" else 2, "lo")):
                        sp.dma_start(heads[QUAD * quad:QUAD * (quad + 1), :, j, :],
                                     part[n, h][rows]).then_inc(spread[n][par], 16)
                sp.wait_ge(spread[n][par], dma_round(g, k) * 16 * 2 * HC)
                if n == "q":
                    sp.dma_start(t[2 * QUAD:4 * QUAD], t[0:2 * QUAD]).then_inc(stacked[n][par], 16)
                else:
                    sp.dma_start(t[QUAD:2 * QUAD], t[0:QUAD]).then_inc(stacked[n][par], 16)
                    sp.dma_start(t[3 * QUAD:4 * QUAD], t[2 * QUAD:3 * QUAD]).then_inc(stacked[n][par], 16)

            def store(g, b):
                sp.wait_ge(ln_done, batch(g, b) + 1)
                sp.dma_start(out[batch(g, b)], y[b][:]).then_inc(stored[b], 16)

            def group(g, par, k):
                first = isinstance(g, int) and g == 0
                if not first:
                    store(g - 1, 0)
                if has_x_next2(g):
                    sp.wait_ge(xo_done, batch(g, GB) if isinstance(g, int) and g < 2 else xo_no(g - 2, 7) + 1)
                    sp.wait_ge(res_made, batch(g, GB))
                    load_x(g + 2, par)
                if has_next(g):
                    if not first:
                        sp.wait_ge(mask_made, g)
                    load_adj(g + 1, 1 - par)
                    stack("q", g + 1, 1 - par, k + par)
                    stack("k", g + 1, 1 - par, k + par)
                if not first:
                    store(g - 1, 1)

            load_x(0, 0)
            load_w(0, Wq)
            sp.dma_start(b_qk[:, 0], bq.rearrange("(c p) -> p c", p=P), allow_slow_non_contiguous=True).then_inc(bias_loaded, 16)
            sp.dma_start(b_qk[:, 1], bk.rearrange("(c p) -> p c", p=P), allow_slow_non_contiguous=True).then_inc(bias_loaded, 16)
            sp.dma_start(b_v[:], bv.rearrange("(c p) -> p c", p=P), allow_slow_non_contiguous=True).then_inc(bias_loaded, 16)
            sp.dma_start(b_out[:], bo.partition_broadcast(P)).then_inc(bias_loaded, 16)
            load_x(1, 1)
            load_w(1, Wk)
            load_adj(0, 0)
            for i, w in ((2, Wv), (3, Wo)):
                sp.wait_ge(w_hi_made, i - 1)
                sp.wait_ge(w_lo_made, i - 1)
                load_w(i, w)
            stack("q", 0, 0, 0)
            stack("k", 0, 0, 0)
            all_groups(sp, group)
            store(LAST, 0)
            store(LAST, 1)
            for b in range(GB):
                sp.wait_ge(stored[b], 16 * NG)

        @block.gpsimd
        def _(pool):
            def residual(g, b, par, k):
                pool.wait_ge(x_loaded[par], 16 * dma_round(g, k))
                if not isinstance(g, int) or g >= 2:
                    pool.wait_ge(y_done, batch(g - 2, b) + 1)
                pool.tensor_tensor(x_res[par][:, b], x_in[par][:, b], b_out[:], ALU.add).then_inc(res_made, 1)

            def normalize(g, b):
                n = batch(g, b)
                pool.wait_ge(moments_done, n + 1)
                pool.sem_inc(gpsimd_goes, 1)
                pool.tensor_scalar(minus_mean[b][:], moments[b][:, 0:1], -1.0, 0.0, ALU.mult,
                                   ALU.add).then_inc(ln_small, 1)
                pool.tensor_scalar(var_eps[b][:], moments[b][:, 1:2], 1.0, EPS, ALU.mult,
                                   ALU.add).then_inc(ln_small, 1)
                pool.wait_ge(ln_small, n * 3 + 2)
                pool.tensor_tensor(inv_std[b][:], var_eps[b][:], minus_half[:], ALU.pow).then_inc(ln_small, 1)
                pool.wait_ge(ln_small, n * 3 + 3)
                pool.sem_inc(gpsimd_goes, 1)
                pool.tensor_scalar(y[b][:], y[b][:], minus_mean[b][:], inv_std[b][:], ALU.add,
                                   ALU.mult).then_inc(ln_done, 1)

            def group(g, par, k):
                if has_next(g):
                    residual(g + 1, 0, 1 - par, k + par)
                if not isinstance(g, int) or g > 0:
                    normalize(g - 1, 0)
                    normalize(g - 1, 1)
                if has_next(g):
                    residual(g + 1, 1, 1 - par, k + par)

            pool.memset(ident[:], 0.0).then_inc(const_made, 1)
            pool.wait_ge(const_made, 1)
            pool.affine_select(out=ident[:], in_=ident[:], compare_op=ALU.not_equal, fill=1.0, base=0,
                               pattern=[[-1, P]], channel_multiplier=1).then_inc(const_made, 1)
            pool.memset(minus_half[:], -0.5).then_inc(const_made, 1)
            pool.wait_ge(const_made, 3)
            pool.wait_ge(b_out_made, 1)
            residual(0, 0, 0, 0)
            residual(0, 1, 0, 0)
            all_groups(pool, group)
            normalize(LAST, 0)
            normalize(LAST, 1)

        @block.scalar
        def _(act):
            def high_part(dst, count):
                act.wait_ge(xo_done, count + 1)
                act.activation(dst, xo_ps[:], ACT.Copy).then_inc(xo_hi, 1)

            def high_part_x(count, g, b, par):
                if not isinstance(g, int) or g >= 2:
                    act.wait_ge(bank_done, bank_no(g - 3, 7) + 1)
                high_part(xT_hi[par][:, :, b * S:(b + 1) * S], count)

            def high_part_attn(count, last_y):
                if not isinstance(last_y, int) or last_y > 0:
                    act.wait_ge(bank_done, last_y)
                high_part(aT_hi[:], count)

            def high_part_bank(g, s, par, k):
                kind, i = TASKS[s]
                act.wait_ge(bank_done, bank_no(g, s) + 1)
                src = proj_ps[bank_of(g, s)]
                if kind == V:
                    if not isinstance(g, int) or g >= 1:
                        act.wait_ge(av_done, unit(g, 0))
                    act.activation(v_hi[1 - par][:, i, :, 0:DH], src[:].rearrange("p (h d) -> p h d", h=HEADS),
                                   ACT.Copy).then_inc(split_hi, 1)
                    return
                if not isinstance(g, int) or g >= 0:
                    act.wait_ge(spread[kind][par], 16 * 2 * HC * dma_round(g, k))
                row = 0 if kind == Q else 1
                for c in range(2):
                    m = 2 * i + c
                    ins = act.activation(part[kind, "hi"][:, m, :], src[:, c * TOK:(c + 1) * TOK], ACT.Identity,
                                         bias=b_qk_up[:, row, m:m + 1])
                ins.then_inc(split_hi, 1)

            def exponentials(g, s):
                u = unit(g, s)
                act.wait_ge(bias_done, u + 1)
                wait(act, pT_done, u - 1)
                for j in range(HC):
                    ins = act.activation(probs[s % 2][:, j], masked[s % 2][:, j], ACT.Exp,
                                         bias=exp_bias[s % 2][:, j:j + 1], scale=EXP_SCALE)
                ins.then_inc(exp_done, 1)

            def high_part_probs(g, s):
                u = unit(g, s)
                act.wait_ge(pT_done, u + 1)
                wait(act, av_done, u - 1)
                act.activation(pT_hi[s % 2][:], pT_ps[s % 2][:], ACT.Copy).then_inc(pT_hi_done, 1)

            def group(g, par, k):
                first = isinstance(g, int) and g == 0
                for s in range(SLOTS):
                    if s == 0 and not first:
                        high_part_bank(g - 1, 7, 1 - par, k)
                    if s > 0 and TASKS[s - 1][0] != Y and has_next(g):
                        high_part_bank(g, s - 1, par, k)
                    if s > 0:
                        high_part_probs(g, s - 1)
                    elif not first:
                        high_part_probs(g - 1, SLOTS - 1)
                    if s == 1 and not first:
                        high_part_attn(xo_no(g, 1), bank_no(g - 1, 6) + 1)
                    if s == 5:
                        high_part_attn(xo_no(g, 5), 0 if first else bank_no(g, 4) + 1)
                    if s in (6, 7) and has_x_next2(g):
                        high_part_x(xo_no(g, s), g + 2, s - 6, par)
                    exponentials(g, s)

            high_part_x(0, 0, 0, 0)
            high_part_x(1, 0, 1, 0)
            act.wait_ge(ones_made, 4)
            for i, n in enumerate("qkvo"):
                act.wait_ge(w_loaded[i], 16)
                act.activation(w_hi[n][:], w_raw[:, i % 2], ACT.Copy,
                               scale=1.0 if n == "o" else UP).then_inc(w_hi_made, 1)
                if i == 0:
                    high_part_x(2, 1, 0, 1)
                    high_part_x(3, 1, 1, 1)
                    act.wait_ge(bias_made, 1)
                elif i < 3:
                    high_part_bank(-1, 2 * i - 2, 1, 0)
                    high_part_bank(-1, 2 * i - 1, 1, 0)
            high_part_bank(-1, 5, 1, 0)
            high_part_bank(-1, 7, 1, 0)
            all_groups(act, group)
            high_part_probs(LAST, SLOTS - 1)
            high_part_attn(xo_no(LAST, 9), bank_no(LAST, 6) + 1)

        @block.vector
        def _(dve):
            def low_part(count, hi, lo):
                dve.wait_ge(xo_hi, count + 1)
                dve.tensor_tensor(lo, xo_ps[:], hi.bitcast(F32), ALU.subtract).then_inc(xo_out, 1)

            def low_part_x(count, b, par):
                cols = slice(b * S, (b + 1) * S)
                low_part(count, xT_hi[par][:, :, cols], xT_lo[par][:, :, cols])

            def low_part_bank(g, s, par):
                kind, i = TASKS[s]
                dve.wait_ge(split_hi, split_no(g, s) + 1)
                src = proj_ps[bank_of(g, s)]
                if kind == V:
                    dve.tensor_tensor(v_lo[1 - par][:, i, :, 0:DH], src[:].rearrange("p (h d) -> p h d", h=HEADS),
                                      v_hi[1 - par][:, i, :, 0:DH], ALU.subtract).then_inc(bank_out, 1)
                    return
                row = 0 if kind == Q else 1
                for c in range(2):
                    m = 2 * i + c
                    ins = dve.scalar_tensor_tensor(out=part[kind, "lo"][:, m, :], in0=src[:, c * TOK:(c + 1) * TOK],
                                                   scalar=b_qk_up[:, row, m:m + 1], in1=part[kind, "hi"][:, m, :],
                                                   op0=ALU.add, op1=ALU.subtract)
                ins.then_inc(bank_out, 1)

            def low_part_probs(g, s):
                dve.wait_ge(pT_hi_done, unit(g, s) + 1)
                dve.tensor_tensor(pT_lo[s % 2][:], pT_ps[s % 2][:], pT_hi[s % 2][:], ALU.subtract).then_inc(pT_out, 1)

            def masked_max(g, s, par):
                u = unit(g, s)
                dve.wait_ge(score_done, u + 1)
                wait(dve, exp_done, u - 1)
                if s == 0:
                    dve.wait_ge(mask_made, g + 1)
                dve.sem_inc(vector_goes, 1)
                for j in range(HC):
                    ins = dve.tensor_tensor_reduce(masked[s % 2][:, j], score_ps[s % 2][:, j], mask[par][:, s // KC],
                                                   1.0, -3.0e38, ALU.add, ALU.max, row_max[s % 2][:, j:j + 1])
                ins.then_inc(max_done, 1)
                dve.wait_ge(max_done, u + 1)
                dve.tensor_scalar(exp_bias[s % 2][:], row_max[s % 2][:], -EXP_SCALE, EXP_SHIFT, ALU.mult,
                                  ALU.add).then_inc(bias_done, 1)

            def head_norm(g, s):
                u = unit(g, s)
                b, c = s // KC, s % KC
                dve.wait_ge(av_done, u + 1)
                dve.reciprocal(inv_sum[s % 2][:], av_view[:, :, DH]).then_inc(inv_done, 1)
                dve.wait_ge(inv_done, u + 1)
                if c == 0 and (not isinstance(g, int) or g > 0):
                    dve.wait_ge(xo_done, xo_no(g - 1, 5) + 1 if b == 0 else xo_no(g, 1) + 1)
                dve.tensor_tensor(attn[b][:, c * P:(c + 1) * P].rearrange("p (h d) -> p h d", h=HC),
                                  av_view[:, :, 0:DH],
                                  inv_sum[s % 2][:].unsqueeze(2).to_broadcast([P, HC, DH]),
                                  ALU.mult).then_inc(attn_done, 1)

            def sum_and_moments(g, b, bank, par):
                n = batch(g, b)
                dve.wait_ge(bank_done, bank_no(*bank) + 1)
                dve.wait_ge(res_made, n + 1)
                if not isinstance(g, int) or g > 0:
                    dve.wait_ge(stored[b], 16 * g)
                dve.tensor_tensor(y[b][:], proj_ps[bank_of(*bank)][:], x_res[par][:, b], ALU.add).then_inc(bank_out, 1)
                dve.wait_ge(bank_out, bank_no(*bank) + 1)
                dve.bn_stats(stats[b][:], y[b][:]).then_inc(y_done, 1)
                dve.wait_ge(y_done, n + 1)
                if not isinstance(g, int) or g > 0:
                    dve.wait_ge(ln_done, batch(g - 1, b) + 1)
                dve.sem_inc(vector_goes, 1)
                dve.bn_aggr(moments[b][:], stats[b][:]).then_inc(moments_done, 1)

            def make_mask(g, par, k):
                dve.wait_ge(adj_loaded[par], 16 * dma_round(g, k))
                if not isinstance(g, int) or g >= 2:
                    dve.wait_ge(max_done, unit(g - 1, 0))
                dve.tensor_scalar(mask[par][:], adj_in[par][:], 0.0, MASKED, ALU.is_equal,
                                  ALU.mult).then_inc(mask_made, 1)

            def group(g, par, k):
                first = isinstance(g, int) and g == 0
                nxt = 1 - par
                for s in range(SLOTS):
                    if s >= 2:
                        head_norm(g, s - 2)
                    elif not first:
                        head_norm(g - 1, SLOTS - 2 + s)
                    masked_max(g, s, par)
                    if s == 1 and not first:
                        low_part(xo_no(g, 1), aT_hi[:], aT_lo[:])
                    if s == 5:
                        low_part(xo_no(g, 5), aT_hi[:], aT_lo[:])
                    if s in (6, 7) and has_x_next2(g):
                        low_part_x(xo_no(g, s), s - 6, par)
                    if s > 0:
                        low_part_probs(g, s - 1)
                    elif not first:
                        low_part_probs(g - 1, SLOTS - 1)
                    if s == 0 and not first:
                        low_part_bank(g - 1, 7, nxt)
                    if s > 0 and TASKS[s - 1][0] != Y and has_next(g):
                        low_part_bank(g, s - 1, par)
                    if s == 5 and not first:
                        sum_and_moments(g - 1, 1, (g, 4), nxt)
                    if s == 7:
                        sum_and_moments(g, 0, (g, 6), par)
                    if s == 4 and has_next(g):
                        make_mask(g + 1, nxt, k + par)

            for i in range(2):
                dve.memset(v_hi[i][:, :, :, DH:VC], UP).then_inc(ones_made, 1)
                dve.memset(v_lo[i][:, :, :, DH:VC], 0.0).then_inc(ones_made, 1)
            low_part_x(0, 0, 0)
            low_part_x(1, 1, 0)
            for i, n in enumerate("qkvo"):
                dve.wait_ge(w_hi_made, i + 1)
                dve.scalar_tensor_tensor(out=w_lo[n][:].rearrange("p c n -> p (c n)"),
                                         in0=w_raw[:, i % 2].rearrange("p c n -> p (c n)"),
                                         scalar=1.0 if n == "o" else UP,
                                         in1=w_hi[n][:].bitcast(F32).rearrange("p c n -> p (c n)"),
                                         op0=ALU.mult, op1=ALU.subtract).then_inc(w_lo_made, 1)
                if i == 0:
                    low_part_x(2, 0, 1)
                    low_part_x(3, 1, 1)
                    dve.wait_ge(bias_loaded, 16 * 4)
                    dve.tensor_scalar(b_qk_up[:], b_qk[:], UP, None, ALU.mult).then_inc(bias_made, 1)
                    dve.tensor_copy(b_v_wide[:], b_v[:].unsqueeze(2).to_broadcast([P, KC, P])).then_inc(bias_made, 1)
                    dve.wait_ge(bias_made, 1)
                elif i < 3:
                    low_part_bank(-1, 2 * i - 2, 1)
                    low_part_bank(-1, 2 * i - 1, 1)
            make_mask(0, 0, 0)
            low_part_bank(-1, 5, 1)
            low_part_bank(-1, 7, 1)
            dve.wait_ge(b_out_mm, 1)
            dve.tensor_tensor(b_out[:], av_ps[:], b_out[:], ALU.add).then_inc(b_out_made, 1)
            all_groups(dve, group)
            head_norm(LAST, SLOTS - 2)
            low_part_probs(LAST, SLOTS - 1)
            head_norm(LAST, SLOTS - 1)
            low_part(xo_no(LAST, 9), aT_hi[:], aT_lo[:])
            sum_and_moments(LAST, 1, (LAST, 8), LAST % 2)

        @block.tensor
        def _(pe):
            def mm(dst, lhsT, rhs, first, last):
                return pe.matmul(dst, lhsT, rhs, start=first, stop=last)

            def transpose_x(count, g, b, par, k):
                pe.wait_ge(x_loaded[par], 16 * dma_round(g, k))
                wait(pe, xo_out, count)
                for c in range(KC):
                    ins = pe.transpose(xo_ps[:, c], x_in[par][:, b, c * P:(c + 1) * P], ident[:])
                ins.then_inc(xo_done, 1)

            def transpose_attn(count, b, last_unit):
                pe.wait_ge(attn_done, last_unit + 1)
                pe.wait_ge(xo_out, count)
                for c in range(KC):
                    ins = pe.transpose(xo_ps[:, c], attn[b][:, c * P:(c + 1) * P], ident[:])
                ins.then_inc(xo_done, 1)

            def qk_bank(kind, half, dst, par):
                for c in range(2):
                    cols = slice((2 * half + c) * P, (2 * half + c + 1) * P)
                    o = dst[:, c * TOK:(c + 1) * TOK]
                    for ki in range(KC):
                        hi, lo = w_hi[kind][:, ki, cols], w_lo[kind][:, ki, cols]
                        mm(o, hi, xT_hi[par][:, ki], ki == 0, False)
                        mm(o, hi, xT_lo[par][:, ki], False, False)
                        ins = mm(o, lo, xT_hi[par][:, ki], False, ki == KC - 1)
                return ins

            def row_bank(dst, a_hi, a_lo, n, cols):
                for ki in range(KC):
                    mm(dst[:], a_hi[:, ki, cols], w_hi[n][:, ki], ki == 0, False)
                    mm(dst[:], a_hi[:, ki, cols], w_lo[n][:, ki], False, False)
                    ins = mm(dst[:], a_lo[:, ki, cols], w_hi[n][:, ki], False, ki == KC - 1)
                return ins

            def bank(g, s, par):
                kind, i = TASKS[s]
                dst = proj_ps[bank_of(g, s)]
                wait(pe, bank_out, bank_no(g, s) - 1)
                if kind in (Q, K):
                    ins = qk_bank(kind, i, dst, par)
                elif kind == V:
                    ins = row_bank(dst, xT_hi[par], xT_lo[par], "v", slice(i * S, (i + 1) * S))
                else:
                    ins = row_bank(dst, aT_hi, aT_lo, "o", slice(0, S))
                ins.then_inc(bank_done, 1)

            def scores(g, s, par, k):
                u = unit(g, s)
                b, c = s // KC, s % KC
                if s == 0:
                    pe.wait_ge(stacked["q"][par], 16 * dma_round(g, k))
                    pe.wait_ge(stacked["k"][par], 32 * dma_round(g, k))
                wait(pe, max_done, u - 1)
                toks = slice(b * S, (b + 1) * S)
                for j in range(HC):
                    h = HC * c + j
                    ins = mm(score_ps[s % 2][:, j], stacks["q"][par][:, h, toks], stacks["k"][par][:, h, toks],
                             True, True)
                ins.then_inc(score_done, 1)

            def transpose_probs(g, s):
                u = unit(g, s)
                pe.wait_ge(exp_done, u + 1)
                wait(pe, pT_out, u - 1)
                for j in range(HC):
                    ins = pe.transpose(pT_ps[s % 2][:, j], probs[s % 2][:, j], ident[:])
                ins.then_inc(pT_done, 1)

            def attend(g, s, par):
                u = unit(g, s)
                b, c = s // KC, s % KC
                pe.wait_ge(pT_out, u + 1)
                wait(pe, attn_done, u)
                if c == 0:
                    pe.wait_ge(bank_out, bank_no(g - 1, 5 if b == 0 else 7) + 1)
                for j in range(HC):
                    h = HC * c + j
                    o = av_view[:, j, 0:VC]
                    mm(o, pT_hi[s % 2][:, j], v_hi[par][:, b, h, 0:VC], True, False)
                    mm(o, pT_hi[s % 2][:, j], v_lo[par][:, b, h, 0:VC], False, False)
                    ins = mm(o, pT_lo[s % 2][:, j], v_hi[par][:, b, h, 0:VC], False, True)
                ins.then_inc(av_done, 1)

            def group(g, par, k):
                first = isinstance(g, int) and g == 0
                nxt = 1 - par
                for s in range(SLOTS):
                    scores(g, s, par, k)
                    if s > 0:
                        transpose_probs(g, s - 1)
                    elif not first:
                        transpose_probs(g - 1, SLOTS - 1)
                    if s == 1 and not first:
                        transpose_attn(xo_no(g, 1), 1, unit(g - 1, SLOTS - 1))
                    if s == 5:
                        transpose_attn(xo_no(g, 5), 0, unit(g, 3))
                    if s in (6, 7) and has_x_next2(g):
                        transpose_x(xo_no(g, s), g + 2, s - 6, par, k + 1)
                    if TASKS[s][0] == Y:
                        if not (s == 4 and first):
                            pe.wait_ge(xo_out, (xo_no(g, 1) if s == 4 else xo_no(g, 5)) + 1)
                            bank(g, s, None)
                    elif has_next(g):
                        if s == 0:
                            pe.wait_ge(xo_out, 4 if first else xo_no(g - 1, 7) + 1)
                        bank(g, s, nxt)
                    if s > 0:
                        attend(g, s - 1, par)
                    elif not first:
                        attend(g - 1, SLOTS - 1, nxt)

            pe.wait_ge(const_made, 2)
            for g in range(2):
                for b in range(GB):
                    transpose_x(g * GB + b, g, b, g, 0)
            pe.wait_ge(xo_out, 2)
            for s in SPLIT_RANK:
                w = "qkv".index(TASKS[s][0])
                pe.wait_ge(w_hi_made, w + 1)
                pe.wait_ge(w_lo_made, w + 1)
                bank(-1, s, 0)
            pe.wait_ge(w_loaded[3], 16)
            pe.wait_ge(bias_made, 2)
            for ki in range(KC):
                ins = mm(av_ps[:], b_v_wide[:, ki], w_raw[:, 1, ki], ki == 0, ki == KC - 1)
            ins.then_inc(b_out_mm, 1)
            pe.wait_ge(b_out_made, 1)
            pe.wait_ge(w_hi_made, 4)
            pe.wait_ge(w_lo_made, 4)
            pe.wait_ge(ones_made, 4)
            all_groups(pe, group)
            transpose_probs(LAST, SLOTS - 1)
            attend(LAST, SLOTS - 1, LAST % 2)
            transpose_attn(xo_no(LAST, 9), 1, unit(LAST, SLOTS - 1))
            pe.wait_ge(xo_out, xo_no(LAST, 9) + 1)
            bank(LAST, 8, None)


_INS = ["x", "adj", "L0_gnn_Wq", "L0_gnn_bq", "L0_gnn_Wk", "L0_gnn_bk", "L0_gnn_Wv", "L0_gnn_bv", "L0_gnn_Wo",
        "L0_gnn_bo"]


def kernel(**inputs):
    import numpy as np
    import concourse.bacc as bacc
    from concourse.bass_utils import run_bass_kernel_spmd

    nc = bacc.Bacc("TRN2", target_bir_lowering=False, num_devices=1)
    arrays, args = {}, []
    for name in _INS:
        a = np.ascontiguousarray(inputs[name])
        arrays[f"in_{name}"] = a
        args.append(nc.dram_tensor(f"in_{name}", a.shape, mybir.dt.from_np(a.dtype), kind="ExternalInput").ap())
    out = nc.dram_tensor("out", inputs["x"].shape, F32, kind="ExternalOutput").ap()
    build_program(nc, *args, out)
    return run_bass_kernel_spmd(nc, [arrays], core_ids=[0]).results[0]["out"]
```

```python
import math
from contextlib import ExitStack

import concourse.bass as bass
from concourse import mybir

F32 = mybir.dt.float32
F32R = mybir.dt.float32r
F16 = mybir.dt.float16
I32 = mybir.dt.int32
ALU = mybir.AluOpType
ACT = mybir.ActivationFunctionType
AX = mybir.AxisListType

P = 128
HEADS = 16
UP = 16.0
P_UP = 10
MASKED = -1e30
EPS = 1e-5
GB = 2
QUAD = 32


def build_program(nc, x_rows, x_cols, adj, w_dram, b_cols, bo, out):
    B, S, D = out.shape
    DH = D // HEADS
    KC = D // P
    HC = HEADS // KC
    NG = B // GB
    SLOTS = GB * KC
    TOK = GB * S
    V_LO, V_HI, V_ONE = 0, DH, 2 * DH
    VC = 2 * DH + 1
    VS = 2 * DH + 2
    assert S == P and DH == QUAD and KC == 4 and GB == 2 and NG % 2 == 0 and NG >= 6
    EXP_SCALE = 1.0 / (UP * UP * math.sqrt(DH))
    EXP_SHIFT = P_UP * math.log(2.0)
    LAST = NG - 1

    Q, K, V, Y = "q", "k", "v", "y"
    TASKS = {0: (Q, 0), 1: (Q, 1), 2: (K, 0), 3: (K, 1), 4: (Y, 1), 5: (V, 0), 6: (V, 1), 7: (Y, 0), 8: (Y, 1)}
    SPLIT_RANK = {0: 0, 1: 1, 2: 2, 3: 3, 5: 4, 6: 5}
    N_SPLIT = len(SPLIT_RANK)

    def unit(g, s):
        return g * SLOTS + s

    def bank_no(g, s):
        if isinstance(g, int) and g == -1:
            return SPLIT_RANK[s]
        if isinstance(g, int) and g == 0:
            return N_SPLIT + s - (1 if s > 4 else 0)
        if isinstance(g, int) and g == LAST:
            return bank_no(LAST - 1, SLOTS - 1) + {4: 1, 7: 2, 8: 3}[s]
        return g * SLOTS + N_SPLIT - 1 + s

    def bank_of(g, s):
        return (bank_no(g, s) if isinstance(g, int) else N_SPLIT - 1 + s) % 2

    def split_no(g, s):
        return (g + 1) * N_SPLIT + SPLIT_RANK[s]

    X_SLOTS = (3, 7)

    def aT_no(g, s):
        return g * GB - 1 + {1: 0, 5: 1, 9: 2}[s]

    def x_half_no(g, h):
        return g * 2 + h

    def batch(g, b):
        return g * GB + b

    def dma_round(g, k):
        return (g // 2 if isinstance(g, int) else k) + 1

    def wait(eng, sem, value):
        if not isinstance(value, int) or value > 0:
            eng.wait_ge(sem, value)

    def has_next(g):
        return not isinstance(g, int) or g < LAST

    def has_x_next2(g):
        return not isinstance(g, int) or g < LAST - 1

    def all_groups(eng, group):
        group(0, 0, 0)
        group(1, 1, 0)
        with eng.Fori(1, NG // 2 - 1) as k:
            group(2 * k, 0, k)
            group(2 * k + 1, 1, k)
        group(NG - 2, 0, NG // 2 - 1)
        group(NG - 1, 1, NG // 2 - 1)

    with ExitStack() as ctx:
        def sb(name, shape, dt):
            return ctx.enter_context(nc.sbuf_tensor(name, shape, dt))

        def ps(name, shape, dt):
            return ctx.enter_context(nc.psum_tensor(name, shape, dt))

        def sem(name):
            return ctx.enter_context(nc.semaphore(name))

        w_raw = sb("w_raw", [P, 2, KC, D], F32)
        w_hi = {n: sb(f"w{n}_hi", [P, KC, D], F32R) for n in "qkvo"}
        w_lo = {n: sb(f"w{n}_lo", [P, KC, D], F32R) for n in "qkvo"}
        b_raw = sb("b_raw", [P, 3, KC], F32)
        b_qk_up = sb("b_qk_up", [P, 2, KC], F32)
        b_v_wide = sb("b_v_wide", [P, KC, P], F32)
        b_out = sb("b_out", [P, D], F32)
        ident = sb("ident", [P, P], F32)
        minus_half = sb("minus_half", [P, 1], F32)
        x_in = [sb(f"x_in{i}", [P, GB, D], F32) for i in range(2)]
        x_res = [sb(f"x_res{i}", [P, GB, D], F32) for i in range(2)]
        adj_in = [sb(f"adj_in{i}", [P, GB, S], I32) for i in range(2)]
        mask = [sb(f"mask{i}", [P, GB, S], F32) for i in range(2)]
        xT_raw = sb("xT_raw", [P, KC, TOK], F32)
        xT_hi = [sb(f"xT_hi{i}", [P, KC, TOK], F32R) for i in range(2)]
        xT_lo = [sb(f"xT_lo{i}", [P, KC, TOK], F32R) for i in range(2)]
        part = {(n, h): sb(f"{n}T_{h}", [P, KC, TOK], F16) for n in "qk" for h in ("hi", "lo")}
        stacks = {n: [sb(f"{n}_stack{i}", [P, HEADS, TOK], F16) for i in range(2)] for n in "qk"}
        v_parts = [sb(f"v_parts{i}", [P, GB, HEADS, VS], F16) for i in range(2)]
        masked = [sb(f"masked{i}", [P, HC, S], F32) for i in range(2)]
        row_max = [sb(f"row_max{i}", [P, HC], F32) for i in range(2)]
        exp_bias = [sb(f"exp_bias{i}", [P, HC], F32) for i in range(2)]
        probs = [sb(f"probs{i}", [P, HC, S], F32) for i in range(2)]
        pT_hi = [sb(f"pT_hi{i}", [P, HC, S], F16) for i in range(2)]
        pT_lo = [sb(f"pT_lo{i}", [P, HC, S], F16) for i in range(2)]
        attn_parts = [sb(f"attn_parts{i}", [P, HC, 2 * DH], F32) for i in range(2)]
        inv_sum = [sb(f"inv_sum{i}", [P, HC], F32) for i in range(2)]
        attn = [sb(f"attn{i}", [P, D], F32) for i in range(2)]
        aT_hi = sb("aT_hi", [P, KC, S], F32R)
        aT_lo = sb("aT_lo", [P, KC, S], F32R)
        y = [sb(f"y{i}", [P, D], F32) for i in range(2)]
        stats = [sb(f"stats{i}", [P, 6], F32) for i in range(2)]
        moments = [sb(f"moments{i}", [P, 2], F32) for i in range(2)]
        minus_mean = [sb(f"minus_mean{i}", [P, 1], F32) for i in range(2)]
        var_eps = [sb(f"var_eps{i}", [P, 1], F32) for i in range(2)]
        inv_std = [sb(f"inv_std{i}", [P, 1], F32) for i in range(2)]

        score_ps = [ps(f"score_ps{i}", [P, HC, S], F32) for i in range(2)]
        pT_ps = [ps(f"pT_ps{i}", [P, HC, S], F32) for i in range(2)]
        proj_ps = [ps(f"proj_ps{i}", [P, D], F32) for i in range(2)]
        aT_ps = ps("aT_ps", [P, KC, P], F32)
        av_ps = ps("av_ps", [P, D], F32)
        av_view = av_ps[:, 0:HC * VS].rearrange("p (h c) -> p h c", h=HC)

        xT_loaded = sem("xT_loaded")
        x_loaded = [sem(f"x_loaded{i}") for i in range(2)]
        adj_loaded = [sem(f"adj_loaded{i}") for i in range(2)]
        w_loaded = [sem(f"w_loaded{i}") for i in range(4)]
        bias_loaded = sem("bias_loaded")
        spread = {n: [sem(f"{n}_spread{i}") for i in range(2)] for n in "qk"}
        stacked = {n: [sem(f"{n}_stacked{i}") for i in range(2)] for n in "qk"}
        stored = [sem(f"stored{i}") for i in range(2)]
        const_made = sem("const_made")
        ones_made = sem("ones_made")
        w_hi_made = sem("w_hi_made")
        w_lo_made = sem("w_lo_made")
        bias_made = sem("bias_made")
        b_out_mm = sem("b_out_mm")
        b_out_made = sem("b_out_made")
        aT_done = sem("aT_done")
        bank_done = sem("bank_done")
        score_done = sem("score_done")
        pT_done = sem("pT_done")
        av_done = sem("av_done")
        x_hi_done = sem("x_hi_done")
        aT_hi_done = sem("aT_hi_done")
        split_hi = sem("split_hi")
        exp_done = sem("exp_done")
        pT_hi_done = sem("pT_hi_done")
        x_lo_done = sem("x_lo_done")
        aT_out = sem("aT_out")
        split_out = sem("split_out")
        mask_made = sem("mask_made")
        max_done = sem("max_done")
        bias_done = sem("bias_done")
        pT_out = sem("pT_out")
        inv_done = sem("inv_done")
        norm_done = sem("norm_done")
        y_summed = sem("y_summed")
        stats_done = sem("stats_done")
        moments_done = sem("moments_done")
        attn_done = sem("attn_done")
        res_made = sem("res_made")
        ln_small = sem("ln_small")
        ln_done = sem("ln_done")
        vector_goes = sem("vector_goes")
        gpsimd_goes = sem("gpsimd_goes")


        block = ctx.enter_context(nc.Block())

        @block.sync
        def _(sp):
            def load_x(g, par):
                sp.dma_start(x_in[par][:], x_rows[g]).then_inc(x_loaded[par], 16)

            def load_xT(g):
                sp.dma_start(xT_raw[:], x_cols[g]).then_inc(xT_loaded, 16)

            def load_adj(g, par):
                sp.dma_start(adj_in[par][:], adj[g]).then_inc(adj_loaded[par], 16)

            def load_w(i):
                sp.dma_start(w_raw[:, i % 2], w_dram[i]).then_inc(w_loaded[i], 16)

            def stack(n, g, par, k):
                if n == "q" and (not isinstance(g, int) or g >= 2):
                    sp.wait_ge(score_done, unit(g - 1, 0))
                sp.wait_ge(split_out, split_no(g - 1, 1 if n == "q" else 3) + 1)
                t = stacks[n][par]
                heads = t[:].rearrange("p (c j) t -> p c j t", j=HC)
                for j in range(HC):
                    rows = slice(QUAD * j, QUAD * (j + 1))
                    for quad, h in ((0, "hi"), (1 if n == "q" else 2, "lo")):
                        sp.dma_start(heads[QUAD * quad:QUAD * (quad + 1), :, j, :],
                                     part[n, h][rows]).then_inc(spread[n][par], 16)
                sp.wait_ge(spread[n][par], dma_round(g, k) * 16 * 2 * HC)
                if n == "q":
                    sp.dma_start(t[2 * QUAD:4 * QUAD], t[0:2 * QUAD]).then_inc(stacked[n][par], 16)
                else:
                    sp.dma_start(t[QUAD:2 * QUAD], t[0:QUAD]).then_inc(stacked[n][par], 16)
                    sp.dma_start(t[3 * QUAD:4 * QUAD], t[2 * QUAD:3 * QUAD]).then_inc(stacked[n][par], 16)

            def store(g, b):
                sp.wait_ge(ln_done, batch(g, b) + 1)
                sp.dma_start(out[batch(g, b)], y[b][:]).then_inc(stored[b], 16)

            def group(g, par, k):
                first = isinstance(g, int) and g == 0
                if has_x_next2(g):
                    sp.wait_ge(x_lo_done, x_half_no(g + 2, 0))
                    load_xT(g + 2)
                    sp.wait_ge(res_made, batch(g, GB))
                    load_x(g + 2, par)
                if has_next(g):
                    if not first:
                        sp.wait_ge(mask_made, g)
                    load_adj(g + 1, 1 - par)
                if not first:
                    store(g - 1, 0)
                if has_next(g):
                    stack("q", g + 1, 1 - par, k + par)
                    stack("k", g + 1, 1 - par, k + par)
                if not first:
                    store(g - 1, 1)

            load_xT(0)
            load_w(0)
            sp.dma_start(b_raw[:], b_cols[:]).then_inc(bias_loaded, 16)
            load_w(1)
            sp.dma_start(b_out[:], bo.partition_broadcast(P)).then_inc(bias_loaded, 16)
            load_adj(0, 0)
            for i in (2, 3):
                sp.wait_ge(w_hi_made, i - 1)
                sp.wait_ge(w_lo_made, i - 1)
                load_w(i)
            sp.wait_ge(x_lo_done, 2)
            load_xT(1)
            load_x(0, 0)
            load_x(1, 1)
            stack("q", 0, 0, 0)
            stack("k", 0, 0, 0)
            all_groups(sp, group)
            store(LAST, 0)
            store(LAST, 1)
            for b in range(GB):
                sp.wait_ge(stored[b], 16 * NG)

        @block.gpsimd
        def _(pool):
            def residual(g, b, par, k):
                pool.wait_ge(x_loaded[par], 16 * dma_round(g, k))
                if not isinstance(g, int) or g >= 2:
                    pool.wait_ge(y_summed, batch(g - 2, b) + 1)
                pool.tensor_tensor(x_res[par][:, b], x_in[par][:, b], b_out[:], ALU.add).then_inc(res_made, 1)

            def attn_sum(g, s):
                b, c = s // KC, s % KC
                pool.wait_ge(norm_done, unit(g, s) + 1)
                if c == 0 and (not isinstance(g, int) or g > 0):
                    pool.wait_ge(aT_done, aT_no(g - 1, 5) + 1 if b == 0 else aT_no(g, 1) + 1)
                pool.tensor_tensor(attn[b][:, c * P:(c + 1) * P].rearrange("p (h d) -> p h d", h=HC),
                                   attn_parts[s % 2][:, :, V_LO:V_LO + DH], attn_parts[s % 2][:, :, V_HI:V_HI + DH],
                                   ALU.add).then_inc(attn_done, 1)

            def normalize(g, b):
                n = batch(g, b)
                pool.wait_ge(moments_done, n + 1)
                pool.sem_inc(gpsimd_goes, 1)
                pool.tensor_scalar(minus_mean[b][:], moments[b][:, 0:1], -1.0, 0.0, ALU.mult,
                                   ALU.add).then_inc(ln_small, 1)
                pool.tensor_scalar(var_eps[b][:], moments[b][:, 1:2], 1.0, EPS, ALU.mult,
                                   ALU.add).then_inc(ln_small, 1)
                pool.wait_ge(ln_small, n * 3 + 2)
                pool.tensor_tensor(inv_std[b][:], var_eps[b][:], minus_half[:], ALU.pow).then_inc(ln_small, 1)
                pool.wait_ge(ln_small, n * 3 + 3)
                pool.sem_inc(gpsimd_goes, 1)
                pool.tensor_scalar(y[b][:], y[b][:], minus_mean[b][:], inv_std[b][:], ALU.add,
                                   ALU.mult).then_inc(ln_done, 1)

            def group(g, par, k):
                first = isinstance(g, int) and g == 0
                for s in range(SLOTS):
                    if s >= 2:
                        attn_sum(g, s - 2)
                    elif not first:
                        attn_sum(g - 1, SLOTS - 2 + s)
                    if s == 1 and not first:
                        normalize(g - 1, 0)
                    if s == 6 and not first:
                        normalize(g - 1, 1)
                    if s in (3, 7) and has_next(g):
                        residual(g + 1, s // KC, 1 - par, k + par)

            pool.memset(ident[:], 0.0).then_inc(const_made, 1)
            pool.wait_ge(const_made, 1)
            pool.affine_select(out=ident[:], in_=ident[:], compare_op=ALU.not_equal, fill=1.0, base=0,
                               pattern=[[-1, P]], channel_multiplier=1).then_inc(const_made, 1)
            pool.memset(minus_half[:], -0.5).then_inc(const_made, 1)
            pool.wait_ge(const_made, 3)
            pool.wait_ge(b_out_made, 1)
            residual(0, 0, 0, 0)
            residual(0, 1, 0, 0)
            all_groups(pool, group)
            attn_sum(LAST, SLOTS - 2)
            attn_sum(LAST, SLOTS - 1)
            normalize(LAST, 0)
            normalize(LAST, 1)

        @block.scalar
        def _(act):
            def high_part_x(g, h, par):
                act.wait_ge(xT_loaded, 16 * (g + 1))
                if not isinstance(g, int) or g >= 2:
                    act.wait_ge(bank_done, bank_no(g - 3, 6) + 1)
                half = slice(h * KC // 2, (h + 1) * KC // 2)
                act.activation(xT_hi[par][:, half], xT_raw[:, half], ACT.Copy).then_inc(x_hi_done, 1)

            def high_part_attn(count, last_y):
                act.wait_ge(aT_done, count + 1)
                if not isinstance(last_y, int) or last_y > 0:
                    act.wait_ge(bank_done, last_y)
                act.activation(aT_hi[:], aT_ps[:], ACT.Copy).then_inc(aT_hi_done, 1)

            def high_part_bank(g, s, par, k):
                kind, i = TASKS[s]
                act.wait_ge(bank_done, bank_no(g, s) + 1)
                src = proj_ps[bank_of(g, s)]
                if kind == V:
                    if not isinstance(g, int) or g >= 1:
                        act.wait_ge(av_done, unit(g, 0))
                    act.activation(v_parts[1 - par][:, i, :, V_HI:V_HI + DH], src[:].rearrange("p (h d) -> p h d", h=HEADS),
                                   ACT.Copy).then_inc(split_hi, 1)
                    return
                if not isinstance(g, int) or g >= 0:
                    act.wait_ge(spread[kind][par], 16 * 2 * HC * dma_round(g, k))
                row = 0 if kind == Q else 1
                for c in range(2):
                    m = 2 * i + c
                    ins = act.activation(part[kind, "hi"][:, m, :], src[:, c * TOK:(c + 1) * TOK], ACT.Identity,
                                         bias=b_qk_up[:, row, m:m + 1])
                ins.then_inc(split_hi, 1)

            def exponentials(g, s):
                u = unit(g, s)
                act.wait_ge(bias_done, u + 1)
                wait(act, pT_done, u - 1)
                for j in range(HC):
                    ins = act.activation(probs[s % 2][:, j], masked[s % 2][:, j], ACT.Exp,
                                         bias=exp_bias[s % 2][:, j:j + 1], scale=EXP_SCALE)
                ins.then_inc(exp_done, 1)

            def high_part_probs(g, s):
                u = unit(g, s)
                act.wait_ge(pT_done, u + 1)
                wait(act, av_done, u - 1)
                act.activation(pT_hi[s % 2][:], pT_ps[s % 2][:], ACT.Copy).then_inc(pT_hi_done, 1)

            def group(g, par, k):
                first = isinstance(g, int) and g == 0
                for s in range(SLOTS):
                    if s > 0 and TASKS[s - 1][0] != Y and has_next(g):
                        high_part_bank(g, s - 1, par, k)
                    if s > 0:
                        high_part_probs(g, s - 1)
                    elif not first:
                        high_part_probs(g - 1, SLOTS - 1)
                    if s == 2 and not first:
                        high_part_attn(aT_no(g, 1), bank_no(g - 1, 7) + 1)
                    if s == 6:
                        high_part_attn(aT_no(g, 5), 0 if first else bank_no(g, 4) + 1)
                    if s in X_SLOTS and has_x_next2(g):
                        high_part_x(g + 2, s // KC, par)
                    exponentials(g, s)

            for h in range(2):
                high_part_x(0, h, 0)
            act.wait_ge(ones_made, 2)
            for i, n in enumerate("qkvo"):
                act.wait_ge(w_loaded[i], 16)
                act.activation(w_hi[n][:], w_raw[:, i % 2], ACT.Copy,
                               scale=1.0 if n == "o" else UP).then_inc(w_hi_made, 1)
                if i == 0:
                    act.wait_ge(bias_made, 1)
                elif i < 3:
                    high_part_bank(-1, 2 * i - 2, 1, 0)
                    high_part_bank(-1, 2 * i - 1, 1, 0)
            high_part_bank(-1, 5, 1, 0)
            high_part_bank(-1, 6, 1, 0)
            for h in range(2):
                high_part_x(1, h, 1)
            all_groups(act, group)
            high_part_probs(LAST, SLOTS - 1)
            high_part_attn(aT_no(LAST, 9), bank_no(LAST, 7) + 1)

        @block.vector
        def _(dve):
            def low_part_x(g, h, par):
                dve.wait_ge(x_hi_done, x_half_no(g, h) + 1)
                half = slice(h * KC // 2, (h + 1) * KC // 2)
                dve.tensor_tensor(xT_lo[par][:, half], xT_raw[:, half], xT_hi[par][:, half].bitcast(F32),
                                  ALU.subtract).then_inc(x_lo_done, 1)

            def low_part_attn(count):
                dve.wait_ge(aT_hi_done, count + 1)
                dve.tensor_tensor(aT_lo[:], aT_ps[:], aT_hi[:].bitcast(F32), ALU.subtract).then_inc(aT_out, 1)

            def low_part_bank(g, s, par):
                kind, i = TASKS[s]
                dve.wait_ge(split_hi, split_no(g, s) + 1)
                src = proj_ps[bank_of(g, s)]
                if kind == V:
                    dve.tensor_tensor(v_parts[1 - par][:, i, :, V_LO:V_LO + DH],
                                      src[:].rearrange("p (h d) -> p h d", h=HEADS),
                                      v_parts[1 - par][:, i, :, V_HI:V_HI + DH], ALU.subtract).then_inc(split_out, 1)
                    return
                row = 0 if kind == Q else 1
                for c in range(2):
                    m = 2 * i + c
                    ins = dve.scalar_tensor_tensor(out=part[kind, "lo"][:, m, :], in0=src[:, c * TOK:(c + 1) * TOK],
                                                   scalar=b_qk_up[:, row, m:m + 1], in1=part[kind, "hi"][:, m, :],
                                                   op0=ALU.add, op1=ALU.subtract)
                ins.then_inc(split_out, 1)

            def low_part_probs(g, s):
                dve.wait_ge(pT_hi_done, unit(g, s) + 1)
                dve.tensor_tensor(pT_lo[s % 2][:], pT_ps[s % 2][:], pT_hi[s % 2][:], ALU.subtract).then_inc(pT_out, 1)

            def masked_max(g, s, par):
                u = unit(g, s)
                dve.wait_ge(score_done, u + 1)
                wait(dve, exp_done, u - 1)
                if s == 0:
                    dve.wait_ge(mask_made, g + 1)
                dve.sem_inc(vector_goes, 1)
                for j in range(HC):
                    ins = dve.tensor_tensor_reduce(masked[s % 2][:, j], score_ps[s % 2][:, j], mask[par][:, s // KC],
                                                   1.0, -3.0e38, ALU.add, ALU.max, row_max[s % 2][:, j:j + 1])
                ins.then_inc(max_done, 1)
                dve.wait_ge(max_done, u + 1)
                dve.tensor_scalar(exp_bias[s % 2][:], row_max[s % 2][:], -EXP_SCALE, EXP_SHIFT, ALU.mult,
                                  ALU.add).then_inc(bias_done, 1)

            def head_norm(g, s):
                u = unit(g, s)
                dve.wait_ge(av_done, u + 1)
                dve.reciprocal(inv_sum[s % 2][:], av_view[:, :, V_ONE]).then_inc(inv_done, 1)
                dve.wait_ge(inv_done, u + 1)
                wait(dve, attn_done, u - 1)
                dve.tensor_tensor(attn_parts[s % 2][:], av_view[:, :, 0:2 * DH],
                                  inv_sum[s % 2][:].unsqueeze(2).to_broadcast([P, HC, 2 * DH]),
                                  ALU.mult).then_inc(norm_done, 1)

            def y_and_moments(g, b, bank, par):
                n = batch(g, b)
                dve.wait_ge(bank_done, bank_no(*bank) + 1)
                dve.wait_ge(res_made, n + 1)
                if not isinstance(g, int) or g > 0:
                    dve.wait_ge(stored[b], 16 * g)
                dve.tensor_tensor(y[b][:], proj_ps[bank_of(*bank)][:], x_res[par][:, b], ALU.add).then_inc(y_summed, 1)
                dve.wait_ge(y_summed, n + 1)
                dve.bn_stats(stats[b][:], y[b][:]).then_inc(stats_done, 1)
                dve.wait_ge(stats_done, n + 1)
                if not isinstance(g, int) or g > 0:
                    dve.wait_ge(ln_done, batch(g - 1, b) + 1)
                dve.sem_inc(vector_goes, 1)
                dve.bn_aggr(moments[b][:], stats[b][:]).then_inc(moments_done, 1)

            def make_mask(g, par, k):
                dve.wait_ge(adj_loaded[par], 16 * dma_round(g, k))
                if not isinstance(g, int) or g >= 2:
                    dve.wait_ge(max_done, unit(g - 1, 0))
                dve.tensor_scalar(mask[par][:], adj_in[par][:], 0.0, MASKED, ALU.is_equal,
                                  ALU.mult).then_inc(mask_made, 1)

            def group(g, par, k):
                first = isinstance(g, int) and g == 0
                nxt = 1 - par
                for s in range(SLOTS):
                    if s >= 2:
                        head_norm(g, s - 2)
                    elif not first:
                        head_norm(g - 1, SLOTS - 2 + s)
                    masked_max(g, s, par)
                    if s > 0:
                        low_part_probs(g, s - 1)
                    elif not first:
                        low_part_probs(g - 1, SLOTS - 1)
                    if s > 0 and TASKS[s - 1][0] != Y and has_next(g):
                        low_part_bank(g, s - 1, par)
                    if s == 2 and not first or s == 6:
                        low_part_attn(aT_no(g, s - 1))
                    if s in X_SLOTS and has_x_next2(g):
                        low_part_x(g + 2, s // KC, par)
                    if s == 0 and not first:
                        y_and_moments(g - 1, 0, (g - 1, 7), nxt)
                    if s == 5 and not first:
                        y_and_moments(g - 1, 1, (g, 4), nxt)
                    if s == 4 and has_next(g):
                        make_mask(g + 1, nxt, k + par)

            for i in range(2):
                dve.memset(v_parts[i][:, :, :, V_ONE:VC], UP).then_inc(ones_made, 1)
            for h in range(2):
                low_part_x(0, h, 0)
            for i, n in enumerate("qkvo"):
                dve.wait_ge(w_hi_made, i + 1)
                dve.scalar_tensor_tensor(out=w_lo[n][:].rearrange("p c n -> p (c n)"),
                                         in0=w_raw[:, i % 2].rearrange("p c n -> p (c n)"),
                                         scalar=1.0 if n == "o" else UP,
                                         in1=w_hi[n][:].bitcast(F32).rearrange("p c n -> p (c n)"),
                                         op0=ALU.mult, op1=ALU.subtract).then_inc(w_lo_made, 1)
                if i == 0:
                    dve.wait_ge(bias_loaded, 16 * 2)
                    dve.tensor_scalar(b_qk_up[:], b_raw[:, 0:2], UP, None, ALU.mult).then_inc(bias_made, 1)
                    dve.tensor_copy(b_v_wide[:], b_raw[:, 2].unsqueeze(2).to_broadcast([P, KC, P])).then_inc(bias_made, 1)
                    dve.wait_ge(bias_made, 1)
                elif i < 3:
                    low_part_bank(-1, 2 * i - 2, 1)
                    low_part_bank(-1, 2 * i - 1, 1)
            make_mask(0, 0, 0)
            low_part_bank(-1, 5, 1)
            low_part_bank(-1, 6, 1)
            for h in range(2):
                low_part_x(1, h, 1)
            dve.wait_ge(b_out_mm, 1)
            dve.tensor_tensor(b_out[:], av_ps[:], b_out[:], ALU.add).then_inc(b_out_made, 1)
            all_groups(dve, group)
            head_norm(LAST, SLOTS - 2)
            low_part_probs(LAST, SLOTS - 1)
            head_norm(LAST, SLOTS - 1)
            y_and_moments(LAST, 0, (LAST, 7), LAST % 2)
            low_part_attn(aT_no(LAST, 9))
            y_and_moments(LAST, 1, (LAST, 8), LAST % 2)

        @block.tensor
        def _(pe):
            def mm(dst, lhsT, rhs, first, last):
                return pe.matmul(dst, lhsT, rhs, start=first, stop=last)

            def transpose_attn(count, b, last_unit):
                pe.wait_ge(attn_done, last_unit + 1)
                wait(pe, aT_out, count)
                for c in range(KC):
                    ins = pe.transpose(aT_ps[:, c], attn[b][:, c * P:(c + 1) * P], ident[:])
                ins.then_inc(aT_done, 1)

            def qk_bank(kind, half, dst, par):
                for c in range(2):
                    cols = slice((2 * half + c) * P, (2 * half + c + 1) * P)
                    o = dst[:, c * TOK:(c + 1) * TOK]
                    for ki in range(KC):
                        hi, lo = w_hi[kind][:, ki, cols], w_lo[kind][:, ki, cols]
                        mm(o, hi, xT_hi[par][:, ki], ki == 0, False)
                        mm(o, hi, xT_lo[par][:, ki], False, False)
                        ins = mm(o, lo, xT_hi[par][:, ki], False, ki == KC - 1)
                return ins

            def row_bank(dst, a_hi, a_lo, n, cols):
                for ki in range(KC):
                    mm(dst[:], a_hi[:, ki, cols], w_hi[n][:, ki], ki == 0, False)
                    mm(dst[:], a_hi[:, ki, cols], w_lo[n][:, ki], False, False)
                    ins = mm(dst[:], a_lo[:, ki, cols], w_hi[n][:, ki], False, ki == KC - 1)
                return ins

            def bank_before(g, s):
                if s is None or isinstance(g, int) and g == -1 and s == 0:
                    return g, None
                g, s = (g, s - 1) if s > 0 else (g - 1, SLOTS - 1)
                if isinstance(g, int):
                    none = {-1: (4, 7), 0: (4,), LAST: (0, 1, 2, 3, 5, 6)}.get(g, ())
                    if s in none:
                        return bank_before(g, s)
                return g, s

            def bank(g, s, par):
                kind, i = TASKS[s]
                dst = proj_ps[bank_of(g, s)]
                before, slot = bank_before(*bank_before(g, s))
                if slot is None:
                    pass
                elif TASKS[slot][0] == Y:
                    pe.wait_ge(y_summed, batch(before - 1 if slot == 4 else before, TASKS[slot][1]) + 1)
                else:
                    pe.wait_ge(split_out, split_no(before, slot) + 1)
                if kind in (Q, K):
                    ins = qk_bank(kind, i, dst, par)
                elif kind == V:
                    ins = row_bank(dst, xT_hi[par], xT_lo[par], "v", slice(i * S, (i + 1) * S))
                else:
                    ins = row_bank(dst, aT_hi, aT_lo, "o", slice(0, S))
                ins.then_inc(bank_done, 1)

            def scores(g, s, par, k):
                u = unit(g, s)
                b, c = s // KC, s % KC
                if s == 0:
                    pe.wait_ge(stacked["q"][par], 16 * dma_round(g, k))
                    pe.wait_ge(stacked["k"][par], 32 * dma_round(g, k))
                wait(pe, max_done, u - 1)
                toks = slice(b * S, (b + 1) * S)
                for j in range(HC):
                    h = HC * c + j
                    ins = mm(score_ps[s % 2][:, j], stacks["q"][par][:, h, toks], stacks["k"][par][:, h, toks],
                             True, True)
                ins.then_inc(score_done, 1)

            def transpose_probs(g, s):
                u = unit(g, s)
                pe.wait_ge(exp_done, u + 1)
                wait(pe, pT_out, u - 1)
                for j in range(HC):
                    ins = pe.transpose(pT_ps[s % 2][:, j], probs[s % 2][:, j], ident[:])
                ins.then_inc(pT_done, 1)

            def attend(g, s, par):
                u = unit(g, s)
                b, c = s // KC, s % KC
                pe.wait_ge(pT_out, u + 1)
                wait(pe, norm_done, u)
                if c == 0:
                    pe.wait_ge(split_out, split_no(g - 1, 5 + b) + 1)
                for j in range(HC):
                    h = HC * c + j
                    mm(av_view[:, j, 0:VC], pT_hi[s % 2][:, j], v_parts[par][:, b, h, 0:VC], True, False)
                    ins = mm(av_view[:, j, V_HI:VC], pT_lo[s % 2][:, j], v_parts[par][:, b, h, V_HI:VC], False, True)
                ins.then_inc(av_done, 1)

            def group(g, par, k):
                first = isinstance(g, int) and g == 0
                nxt = 1 - par
                for s in range(SLOTS):
                    scores(g, s, par, k)
                    if s > 0:
                        transpose_probs(g, s - 1)
                    elif not first:
                        transpose_probs(g - 1, SLOTS - 1)
                    if TASKS[s][0] == Y:
                        if not (s == 4 and first):
                            pe.wait_ge(aT_out, aT_no(g, 1 if s == 4 else 5) + 1)
                            if s == 7 and first:
                                pe.wait_ge(w_hi_made, 4)
                                pe.wait_ge(w_lo_made, 4)
                            bank(g, s, None)
                    elif has_next(g):
                        if s == 0:
                            pe.wait_ge(x_lo_done, x_half_no(g + 2, 0))
                        bank(g, s, nxt)
                    if s == 1 and not first:
                        transpose_attn(aT_no(g, 1), 1, unit(g - 1, SLOTS - 1))
                    if s == 5:
                        transpose_attn(aT_no(g, 5), 0, unit(g, 3))
                    if s == 1 and first:
                        pe.wait_ge(b_out_made, 1)
                        pe.wait_ge(ones_made, 2)
                    if s > 0:
                        attend(g, s - 1, par)
                    elif not first:
                        attend(g - 1, SLOTS - 1, nxt)

            pe.wait_ge(x_lo_done, 2)
            for s in SPLIT_RANK:
                w = "qkv".index(TASKS[s][0])
                pe.wait_ge(w_hi_made, w + 1)
                pe.wait_ge(w_lo_made, w + 1)
                bank(-1, s, 0)
            pe.wait_ge(w_loaded[3], 16)
            pe.wait_ge(bias_made, 2)
            for ki in range(KC):
                ins = mm(av_ps[:], b_v_wide[:, ki], w_raw[:, 1, ki], ki == 0, ki == KC - 1)
            ins.then_inc(b_out_mm, 1)
            pe.wait_ge(const_made, 2)
            all_groups(pe, group)
            transpose_probs(LAST, SLOTS - 1)
            attend(LAST, SLOTS - 1, LAST % 2)
            transpose_attn(aT_no(LAST, 9), 1, unit(LAST, SLOTS - 1))
            pe.wait_ge(aT_out, aT_no(LAST, 9) + 1)
            bank(LAST, 8, None)


def layouts(x, adj, weights, biases, bo):
    import numpy as np

    B, S, D = x.shape
    KC = D // P
    return {
        "x_rows": x.reshape(B // GB, GB, S, D).transpose(0, 2, 1, 3),
        "x_cols": x.reshape(B // GB, GB * S, KC, P).transpose(0, 3, 2, 1),
        "adj": adj.reshape(B // GB, GB, S, S).transpose(0, 2, 1, 3),
        "weights": np.stack([w.reshape(KC, P, D).transpose(1, 0, 2) for w in weights]),
        "biases": np.stack([b.reshape(KC, P).T for b in biases], axis=1),
        "bo": bo,
    }


def kernel(x, adj, L0_gnn_Wq, L0_gnn_bq, L0_gnn_Wk, L0_gnn_bk, L0_gnn_Wv, L0_gnn_bv, L0_gnn_Wo, L0_gnn_bo):
    import numpy as np
    import concourse.bacc as bacc
    from concourse.bass_utils import run_bass_kernel_spmd

    nc = bacc.Bacc("TRN2", target_bir_lowering=False, num_devices=1)
    x, adj, bo = np.asarray(x), np.asarray(adj), np.asarray(L0_gnn_bo)
    weights = [np.asarray(w) for w in (L0_gnn_Wq, L0_gnn_Wk, L0_gnn_Wv, L0_gnn_Wo)]
    biases = [np.asarray(b) for b in (L0_gnn_bq, L0_gnn_bk, L0_gnn_bv)]
    arrays = {n: np.ascontiguousarray(a) for n, a in layouts(x, adj, weights, biases, bo).items()}
    args = [nc.dram_tensor(n, a.shape, mybir.dt.from_np(a.dtype), kind="ExternalInput").ap()
            for n, a in arrays.items()]
    out = nc.dram_tensor("out", x.shape, F32, kind="ExternalOutput").ap()
    build_program(nc, *args, out)
    return run_bass_kernel_spmd(nc, [arrays], core_ids=[0]).results[0]["out"]
```

```python
import math
from contextlib import ExitStack

import concourse.bass as bass
from concourse import mybir

F32 = mybir.dt.float32
F32R = mybir.dt.float32r
F16 = mybir.dt.float16
I32 = mybir.dt.int32
ALU = mybir.AluOpType
ACT = mybir.ActivationFunctionType
AX = mybir.AxisListType

P = 128
HEADS = 16
UP = 16.0
P_UP = 1024.0
MASKED = -1e30
EPS = 1e-5
GB = 2
QUAD = 32


def build_program(nc, x_rows, x_cols, adj, w_dram, b_cols, bo, out):
    B, S, D = out.shape
    DH = D // HEADS
    KC = D // P
    HC = HEADS // KC
    NG = B // GB
    SLOTS = GB * KC
    TOK = GB * S
    V_LO, V_HI, V_ONE = 0, DH, 2 * DH
    VC = 2 * DH + 1
    VS = 2 * DH + 2
    assert S == P and DH == QUAD and KC == 4 and GB == 2 and NG % 2 == 0 and NG >= 6
    EXP_SCALE = 1.0 / (UP * UP * math.sqrt(DH))
    LAST = NG - 1

    Q, K, V, Y = "q", "k", "v", "y"
    TASKS = {0: (Q, 0), 1: (Q, 1), 2: (K, 0), 3: (K, 1), 4: (Y, 1), 5: (V, 0), 6: (V, 1), 7: (Y, 0), 8: (Y, 1)}
    SPLIT_RANK = {0: 0, 1: 1, 2: 2, 3: 3, 5: 4, 6: 5}
    N_SPLIT = len(SPLIT_RANK)

    def unit(g, s):
        return g * SLOTS + s

    def bank_no(g, s):
        if isinstance(g, int) and g == -1:
            return SPLIT_RANK[s]
        if isinstance(g, int) and g == 0:
            return N_SPLIT + s - (1 if s > 4 else 0)
        if isinstance(g, int) and g == LAST:
            return bank_no(LAST - 1, SLOTS - 1) + {4: 1, 7: 2, 8: 3}[s]
        return g * SLOTS + N_SPLIT - 1 + s

    def bank_of(g, s):
        return (bank_no(g, s) if isinstance(g, int) else N_SPLIT - 1 + s) % 2

    def split_no(g, s):
        return (g + 1) * N_SPLIT + SPLIT_RANK[s]

    X_SLOTS = (2, 4)

    def aT_no(g, s):
        return g * GB - 1 + {1: 0, 5: 1, 9: 2}[s]

    def x_half_no(g, h):
        return g * 2 + h

    def batch(g, b):
        return g * GB + b

    def dma_round(g, k):
        return (g // 2 if isinstance(g, int) else k) + 1

    def wait(eng, sem, value):
        if not isinstance(value, int) or value > 0:
            eng.wait_ge(sem, value)

    def has_next(g):
        return not isinstance(g, int) or g < LAST

    def has_x_next2(g):
        return not isinstance(g, int) or g < LAST - 1

    def all_groups(eng, group, first=None, last=None):
        (first or group)(0, 0, 0)
        group(1, 1, 0)
        with eng.Fori(1, NG // 2 - 1) as k:
            group(2 * k, 0, k)
            group(2 * k + 1, 1, k)
        group(NG - 2, 0, NG // 2 - 1)
        (last or group)(NG - 1, 1, NG // 2 - 1)

    with ExitStack() as ctx:
        def sb(name, shape, dt):
            return ctx.enter_context(nc.sbuf_tensor(name, shape, dt))

        def ps(name, shape, dt):
            return ctx.enter_context(nc.psum_tensor(name, shape, dt))

        def sem(name):
            return ctx.enter_context(nc.semaphore(name))

        w_land = [sb(f"w_land{i}", [P, KC, D], F32) for i in range(2)]
        w_hi = {n: sb(f"w{n}_hi", [P, KC, D], F32R) for n in "qkvo"}
        w_lo = {n: sb(f"w{n}_lo", [P, KC, D], F32R) for n in "qkvo"}
        b_raw = sb("b_raw", [P, 3, KC], F32)
        b_qk_up = sb("b_qk_up", [P, 2, KC], F32)
        b_v_wide = sb("b_v_wide", [P, KC, P], F32)
        b_out = sb("b_out", [P, D], F32)
        ident = sb("ident", [P, P], F32)
        minus_half = sb("minus_half", [P, 1], F32)
        x_in = [sb(f"x_in{i}", [P, GB, D], F32) for i in range(2)]
        x_res = sb("x_res", [P, 2, GB, D], F32)
        w_raw = {"q": w_land[0], "k": w_land[1], "v": x_res[:].rearrange("p i b d -> p (i b) d"), "o": w_land[0]}
        adj_in = [sb(f"adj_in{i}", [P, GB, S], I32) for i in range(2)]
        mask = [sb(f"mask{i}", [P, GB, S], F32) for i in range(2)]
        xT_raw = sb("xT_raw", [P, KC, TOK], F32)
        xT_hi = [sb(f"xT_hi{i}", [P, KC, TOK], F32R) for i in range(2)]
        xT_lo = [sb(f"xT_lo{i}", [P, KC, TOK], F32R) for i in range(2)]
        part = {(n, h): sb(f"{n}T_{h}", [P, KC, TOK], F16) for n in "qk" for h in ("hi", "lo")}
        stacks = {n: [sb(f"{n}_stack{i}", [P, HEADS, TOK], F16) for i in range(2)] for n in "qk"}
        v_parts = [sb(f"v_parts{i}", [P, GB, HEADS, VS], F16) for i in range(2)]
        masked = [sb(f"masked{i}", [P, HC, S], F32) for i in range(2)]
        minus_max = [sb(f"minus_max{i}", [P, HC], F32) for i in range(2)]
        probs = [sb(f"probs{i}", [P, HC, S], F32) for i in range(2)]
        pT_hi = [sb(f"pT_hi{i}", [P, HC, S], F16) for i in range(2)]
        pT_lo = [sb(f"pT_lo{i}", [P, HC, S], F16) for i in range(2)]
        attn_parts = [sb(f"attn_parts{i}", [P, HC, 2 * DH], F32) for i in range(2)]
        inv_sum = [sb(f"inv_sum{i}", [P, HC], F32) for i in range(2)]
        attn = [sb(f"attn{i}", [P, D], F32) for i in range(2)]
        aT_hi = sb("aT_hi", [P, KC, S], F32R)
        aT_lo = sb("aT_lo", [P, KC, S], F32R)
        y = [sb(f"y{i}", [P, D], F32) for i in range(2)]
        stats = [sb(f"stats{i}", [P, 6], F32) for i in range(2)]
        moments = [sb(f"moments{i}", [P, 2], F32) for i in range(2)]
        minus_mean = [sb(f"minus_mean{i}", [P, 1], F32) for i in range(2)]
        var_eps = [sb(f"var_eps{i}", [P, 1], F32) for i in range(2)]
        inv_std = [sb(f"inv_std{i}", [P, 1], F32) for i in range(2)]

        score_ps = [ps(f"score_ps{i}", [P, HC, S], F32) for i in range(2)]
        pT_ps = [ps(f"pT_ps{i}", [P, HC, S], F32) for i in range(2)]
        proj_ps = [ps(f"proj_ps{i}", [P, D], F32) for i in range(2)]
        aT_ps = ps("aT_ps", [P, KC, P], F32)
        b_out_ps = aT_ps[:].rearrange("p c t -> p (c t)")
        av_ps = ps("av_ps", [P, D], F32)
        av_view = av_ps[:, 0:HC * VS].rearrange("p (h c) -> p h c", h=HC)

        xT_loaded = sem("xT_loaded")
        x_loaded = [sem(f"x_loaded{i}") for i in range(2)]
        adj_loaded = [sem(f"adj_loaded{i}") for i in range(2)]
        w_loaded = {n: [sem(f"w{n}_loaded{c}") for c in range(KC if n == "q" else 1)] for n in "qkvo"}
        bias_loaded = sem("bias_loaded")
        bo_loaded = sem("bo_loaded")
        spread = {n: [sem(f"{n}_spread{i}") for i in range(2)] for n in "qk"}
        stacked = {n: [sem(f"{n}_stacked{i}") for i in range(2)] for n in "qk"}
        stored = [sem(f"stored{i}") for i in range(2)]
        const_made = sem("const_made")
        ones_made = sem("ones_made")
        w_hi_made = sem("w_hi_made")
        w_lo_made = sem("w_lo_made")
        bias_made = sem("bias_made")
        b_out_mm = sem("b_out_mm")
        b_out_made = sem("b_out_made")
        aT_done = sem("aT_done")
        bank_done = sem("bank_done")
        score_done = sem("score_done")
        pT_done = sem("pT_done")
        av_done = sem("av_done")
        x_hi_done = sem("x_hi_done")
        aT_hi_done = sem("aT_hi_done")
        split_hi = sem("split_hi")
        exp_done = sem("exp_done")
        pT_hi_done = sem("pT_hi_done")
        x_lo_done = sem("x_lo_done")
        aT_out = sem("aT_out")
        split_out = sem("split_out")
        mask_made = sem("mask_made")
        max_done = sem("max_done")
        pT_out = sem("pT_out")
        inv_done = sem("inv_done")
        norm_done = sem("norm_done")
        y_summed = sem("y_summed")
        stats_done = sem("stats_done")
        moments_done = sem("moments_done")
        attn_done = sem("attn_done")
        res_made = sem("res_made")
        ln_small = sem("ln_small")
        ln_done = sem("ln_done")
        vector_goes = sem("vector_goes")
        gpsimd_goes = sem("gpsimd_goes")


        def low_part_x(eng, g, h, par):
            eng.wait_ge(x_hi_done, x_half_no(g, h) + 1)
            half = slice(h * KC // 2, (h + 1) * KC // 2)
            eng.tensor_tensor(xT_lo[par][:, half], xT_raw[:, half], xT_hi[par][:, half].bitcast(F32),
                              ALU.subtract).then_inc(x_lo_done, 1)

        block = ctx.enter_context(nc.Block())

        @block.sync
        def _(sp):
            def load_x(g, par):
                sp.dma_start(x_in[par][:], x_rows[g]).then_inc(x_loaded[par], 16)

            def load_xT(g):
                sp.dma_start(xT_raw[:], x_cols[g]).then_inc(xT_loaded, 16)

            def load_adj(g, par):
                sp.dma_start(adj_in[par][:], adj[g]).then_inc(adj_loaded[par], 16)

            def load_w(n):
                for c, loaded in enumerate(w_loaded[n]):
                    rows = slice(c, c + 1) if len(w_loaded[n]) > 1 else slice(0, KC)
                    sp.dma_start(w_raw[n][:, rows], w_dram["qkvo".index(n), :, rows]).then_inc(loaded, 16)

            def spread_rows(n, g, par, k):
                if n == "q" and (not isinstance(g, int) or g >= 2):
                    sp.wait_ge(score_done, unit(g - 1, 0))
                sp.wait_ge(split_out, split_no(g - 1, 1 if n == "q" else 3) + 1)
                t = stacks[n][par]
                heads = t[:].rearrange("p (c j) t -> p c j t", j=HC)
                for j in range(HC):
                    rows = slice(QUAD * j, QUAD * (j + 1))
                    for quad, h in ((0, "hi"), (1 if n == "k" else 2, "lo")):
                        sp.dma_start(heads[QUAD * quad:QUAD * (quad + 1), :, j, :],
                                     part[n, h][rows]).then_inc(spread[n][par], 16)

            def copy_rows(n, g, par, k):
                t = stacks[n][par]
                sp.wait_ge(spread[n][par], dma_round(g, k) * 16 * 2 * HC)
                if n == "k":
                    sp.dma_start(t[2 * QUAD:4 * QUAD], t[0:2 * QUAD]).then_inc(stacked[n][par], 16)
                else:
                    sp.dma_start(t[QUAD:2 * QUAD], t[0:QUAD]).then_inc(stacked[n][par], 16)
                    sp.dma_start(t[3 * QUAD:4 * QUAD], t[2 * QUAD:3 * QUAD]).then_inc(stacked[n][par], 16)

            def store(g, b):
                sp.wait_ge(ln_done, batch(g, b) + 1)
                sp.dma_start(out[batch(g, b)], y[b][:]).then_inc(stored[b], 16)

            def group(g, par, k):
                first = isinstance(g, int) and g == 0
                if has_x_next2(g):
                    sp.wait_ge(x_lo_done, x_half_no(g + 2, 0))
                    load_xT(g + 2)
                if has_next(g):
                    if not first:
                        sp.wait_ge(mask_made, g)
                    load_adj(g + 1, 1 - par)
                if not first:
                    store(g - 1, 0)
                if has_next(g):
                    spread_rows("q", g + 1, 1 - par, k + par)
                    copy_rows("q", g + 1, 1 - par, k + par)
                    spread_rows("k", g + 1, 1 - par, k + par)
                    copy_rows("k", g + 1, 1 - par, k + par)
                if not first:
                    store(g - 1, 1)
                if has_x_next2(g):
                    sp.wait_ge(res_made, batch(g, GB))
                    load_x(g + 2, par)

            load_xT(0)
            load_w("q")
            sp.dma_start(b_raw[:], b_cols[:]).then_inc(bias_loaded, 16)
            load_w("k")
            load_w("v")
            sp.wait_ge(x_lo_done, 2)
            load_xT(1)
            load_adj(0, 0)
            sp.wait_ge(w_lo_made, KC)
            load_w("o")
            sp.dma_start(b_out[:], bo.partition_broadcast(P)).then_inc(bo_loaded, 16)
            spread_rows("q", 0, 0, 0)
            spread_rows("k", 0, 0, 0)
            copy_rows("q", 0, 0, 0)
            copy_rows("k", 0, 0, 0)
            load_x(0, 0)
            load_x(1, 1)
            all_groups(sp, group)
            store(LAST, 0)
            store(LAST, 1)
            for b in range(GB):
                sp.wait_ge(stored[b], 16 * NG)

        @block.gpsimd
        def _(pool):
            def residual(g, b, par, k):
                pool.wait_ge(x_loaded[par], 16 * dma_round(g, k))
                if not isinstance(g, int) or g >= 2:
                    pool.wait_ge(y_summed, batch(g - 2, b) + 1)
                pool.tensor_tensor(x_res[:, par, b], x_in[par][:, b], b_out[:], ALU.add).then_inc(res_made, 1)

            def attn_sum(g, s):
                b, c = s // KC, s % KC
                pool.wait_ge(norm_done, unit(g, s) + 1)
                if c == 0 and (not isinstance(g, int) or g > 0):
                    pool.wait_ge(aT_done, aT_no(g - 1, 5) + 1 if b == 0 else aT_no(g, 1) + 1)
                pool.tensor_tensor(attn[b][:, c * P:(c + 1) * P].rearrange("p (h d) -> p h d", h=HC),
                                   attn_parts[s % 2][:, :, V_LO:V_LO + DH], attn_parts[s % 2][:, :, V_HI:V_HI + DH],
                                   ALU.add).then_inc(attn_done, 1)

            def normalize(g, b):
                n = batch(g, b)
                pool.wait_ge(moments_done, n + 1)
                pool.sem_inc(gpsimd_goes, 1)
                pool.tensor_scalar(minus_mean[b][:], moments[b][:, 0:1], -1.0, 0.0, ALU.mult,
                                   ALU.add).then_inc(ln_small, 1)
                pool.tensor_scalar(var_eps[b][:], moments[b][:, 1:2], 1.0, EPS, ALU.mult,
                                   ALU.add).then_inc(ln_small, 1)
                pool.wait_ge(ln_small, n * 3 + 2)
                pool.tensor_tensor(inv_std[b][:], var_eps[b][:], minus_half[:], ALU.pow).then_inc(ln_small, 1)
                pool.wait_ge(ln_small, n * 3 + 3)
                pool.sem_inc(gpsimd_goes, 1)
                pool.tensor_scalar(y[b][:], y[b][:], minus_mean[b][:], inv_std[b][:], ALU.add,
                                   ALU.mult).then_inc(ln_done, 1)

            def group(g, par, k):
                first = isinstance(g, int) and g == 0
                for s in range(SLOTS):
                    if s >= 2:
                        attn_sum(g, s - 2)
                    elif not first:
                        attn_sum(g - 1, SLOTS - 2 + s)
                    if s == 1 and not first:
                        normalize(g - 1, 0)
                    if s == 6 and not first:
                        normalize(g - 1, 1)
                    if s in X_SLOTS and has_x_next2(g):
                        low_part_x(pool, g + 2, X_SLOTS.index(s), par)
                    if s == 5 and first:
                        pool.wait_ge(b_out_made, 1)
                        residual(0, 0, 0, 0)
                        residual(0, 1, 0, 0)
                    if s == 6 and first:
                        residual(1, 0, 1, 0)
                    elif s == 3 and not first and has_next(g) or s == 7 and has_next(g):
                        residual(g + 1, s // KC, 1 - par, k + par)

            pool.memset(ident[:], 0.0).then_inc(const_made, 1)
            pool.wait_ge(const_made, 1)
            pool.affine_select(out=ident[:], in_=ident[:], compare_op=ALU.not_equal, fill=1.0, base=0,
                               pattern=[[-1, P]], channel_multiplier=1).then_inc(const_made, 1)
            pool.memset(minus_half[:], -0.5).then_inc(const_made, 1)
            pool.wait_ge(const_made, 3)
            all_groups(pool, group)
            attn_sum(LAST, SLOTS - 2)
            attn_sum(LAST, SLOTS - 1)
            normalize(LAST, 0)
            normalize(LAST, 1)

        @block.scalar
        def _(act):
            def high_part_x(g, h, par):
                act.wait_ge(xT_loaded, 16 * (g + 1))
                if not isinstance(g, int) or g >= 2:
                    act.wait_ge(bank_done, bank_no(g - 3, 6) + 1)
                half = slice(h * KC // 2, (h + 1) * KC // 2)
                act.activation(xT_hi[par][:, half], xT_raw[:, half], ACT.Copy).then_inc(x_hi_done, 1)

            def high_part_attn(count, last_y):
                act.wait_ge(aT_done, count + 1)
                if not isinstance(last_y, int) or last_y > 0:
                    act.wait_ge(bank_done, last_y)
                act.activation(aT_hi[:], aT_ps[:], ACT.Copy).then_inc(aT_hi_done, 1)

            def high_part_bank(g, s, par, k):
                kind, i = TASKS[s]
                act.wait_ge(bank_done, bank_no(g, s) + 1)
                src = proj_ps[bank_of(g, s)]
                if kind == V:
                    if not isinstance(g, int) or g >= 1:
                        act.wait_ge(av_done, unit(g, 0))
                    act.activation(v_parts[1 - par][:, i, :, V_HI:V_HI + DH],
                                   src[:].rearrange("p (h d) -> p h d", h=HEADS), ACT.Copy).then_inc(split_hi, 1)
                    return
                if not isinstance(g, int) or g >= 0:
                    act.wait_ge(spread[kind][par], 16 * 2 * HC * dma_round(g, k))
                row = 0 if kind == Q else 1
                for c in range(2):
                    m = 2 * i + c
                    ins = act.activation(part[kind, "hi"][:, m, :], src[:, c * TOK:(c + 1) * TOK], ACT.Identity,
                                         bias=b_qk_up[:, row, m:m + 1])
                ins.then_inc(split_hi, 1)

            def exponentials(g, s):
                u = unit(g, s)
                act.wait_ge(max_done, u + 1)
                wait(act, pT_done, u - 1)
                for j in range(HC):
                    ins = act.activation(probs[s % 2][:, j], masked[s % 2][:, j], ACT.Exp,
                                         bias=minus_max[s % 2][:, j:j + 1], scale=-1.0)
                ins.then_inc(exp_done, 1)

            def high_part_probs(g, s):
                u = unit(g, s)
                act.wait_ge(pT_done, u + 1)
                wait(act, av_done, u - 1)
                act.activation(pT_hi[s % 2][:], pT_ps[s % 2][:], ACT.Copy, scale=P_UP).then_inc(pT_hi_done, 1)

            def group(g, par, k):
                first = isinstance(g, int) and g == 0
                for s in range(SLOTS):
                    filled = s if first else s - 1
                    if filled in SPLIT_RANK and has_next(g):
                        high_part_bank(g, filled, par, k)
                    if not has_next(g):
                        exponentials(g, s)
                    if s > 0:
                        high_part_probs(g, s - 1)
                    elif not first:
                        high_part_probs(g - 1, SLOTS - 1)
                    if s == 2 and not first:
                        high_part_attn(aT_no(g, 1), bank_no(g - 1, 7) + 1)
                    if s == 6:
                        high_part_attn(aT_no(g, 5), 0 if first else bank_no(g, 4) + 1)
                    if s in X_SLOTS and has_x_next2(g):
                        high_part_x(g + 2, X_SLOTS.index(s), par)
                    if has_next(g):
                        exponentials(g, s)

            for h in range(2):
                high_part_x(0, h, 0)
            act.wait_ge(ones_made, 2)
            for n in "qkvo":
                for c in range(KC):
                    if c < len(w_loaded[n]):
                        act.wait_ge(w_loaded[n][c], 16)
                    act.activation(w_hi[n][:, c], w_raw[n][:, c], ACT.Copy,
                                   scale=1.0 if n == "o" else UP).then_inc(w_hi_made, 1)
                if n == "k":
                    act.wait_ge(bias_made, 1)
                    high_part_bank(-1, 0, 1, 0)
                    high_part_bank(-1, 1, 1, 0)
                if n == "v":
                    high_part_bank(-1, 2, 1, 0)
                    high_part_bank(-1, 3, 1, 0)
                    for h in range(2):
                        high_part_x(1, h, 1)
                    high_part_bank(-1, 5, 1, 0)
                    high_part_bank(-1, 6, 1, 0)
            all_groups(act, group)
            high_part_probs(LAST, SLOTS - 1)
            high_part_attn(aT_no(LAST, 9), bank_no(LAST, 7) + 1)

        @block.vector
        def _(dve):
            def low_part_attn(count):
                dve.wait_ge(aT_hi_done, count + 1)
                dve.tensor_tensor(aT_lo[:], aT_ps[:], aT_hi[:].bitcast(F32), ALU.subtract).then_inc(aT_out, 1)

            def low_part_bank(g, s, par):
                kind, i = TASKS[s]
                dve.wait_ge(split_hi, split_no(g, s) + 1)
                src = proj_ps[bank_of(g, s)]
                if kind == V:
                    dve.tensor_tensor(v_parts[1 - par][:, i, :, V_LO:V_LO + DH],
                                      src[:].rearrange("p (h d) -> p h d", h=HEADS),
                                      v_parts[1 - par][:, i, :, V_HI:V_HI + DH], ALU.subtract).then_inc(split_out, 1)
                    return
                row = 0 if kind == Q else 1
                for c in range(2):
                    m = 2 * i + c
                    ins = dve.scalar_tensor_tensor(out=part[kind, "lo"][:, m, :], in0=src[:, c * TOK:(c + 1) * TOK],
                                                   scalar=b_qk_up[:, row, m:m + 1], in1=part[kind, "hi"][:, m, :],
                                                   op0=ALU.add, op1=ALU.subtract)
                ins.then_inc(split_out, 1)

            def low_part_probs(g, s):
                dve.wait_ge(pT_hi_done, unit(g, s) + 1)
                dve.scalar_tensor_tensor(out=pT_lo[s % 2][:], in0=pT_ps[s % 2][:], scalar=P_UP, in1=pT_hi[s % 2][:],
                                         op0=ALU.mult, op1=ALU.subtract).then_inc(pT_out, 1)

            def masked_max(g, s, par):
                u = unit(g, s)
                dve.wait_ge(score_done, u + 1)
                wait(dve, exp_done, u - 1)
                if s == 0:
                    dve.wait_ge(mask_made, g + 1)
                dve.sem_inc(vector_goes, 1)
                for j in range(HC):
                    ins = dve.tensor_tensor_reduce(masked[s % 2][:, j], score_ps[s % 2][:, j], mask[par][:, s // KC],
                                                   -EXP_SCALE, 3.0e38, ALU.add, ALU.min,
                                                   minus_max[s % 2][:, j:j + 1])
                ins.then_inc(max_done, 1)

            def head_norm(g, s):
                u = unit(g, s)
                dve.wait_ge(av_done, u + 1)
                dve.reciprocal(inv_sum[s % 2][:], av_view[:, :, V_ONE]).then_inc(inv_done, 1)
                dve.wait_ge(inv_done, u + 1)
                wait(dve, attn_done, u - 1)
                dve.tensor_tensor(attn_parts[s % 2][:], av_view[:, :, 0:2 * DH],
                                  inv_sum[s % 2][:].unsqueeze(2).to_broadcast([P, HC, 2 * DH]),
                                  ALU.mult).then_inc(norm_done, 1)

            def y_and_moments(g, b, bank, par):
                n = batch(g, b)
                dve.wait_ge(bank_done, bank_no(*bank) + 1)
                dve.wait_ge(res_made, n + 1)
                if not isinstance(g, int) or g > 0:
                    dve.wait_ge(stored[b], 16 * g)
                dve.tensor_tensor(y[b][:], proj_ps[bank_of(*bank)][:], x_res[:, par, b], ALU.add).then_inc(y_summed, 1)
                dve.wait_ge(y_summed, n + 1)
                dve.bn_stats(stats[b][:], y[b][:]).then_inc(stats_done, 1)
                dve.wait_ge(stats_done, n + 1)
                if not isinstance(g, int) or g > 0:
                    dve.wait_ge(ln_done, batch(g - 1, b) + 1)
                dve.sem_inc(vector_goes, 1)
                dve.bn_aggr(moments[b][:], stats[b][:]).then_inc(moments_done, 1)

            def make_mask(g, par, k):
                dve.wait_ge(adj_loaded[par], 16 * dma_round(g, k))
                if not isinstance(g, int) or g >= 2:
                    dve.wait_ge(max_done, unit(g - 1, 0))
                dve.tensor_scalar(mask[par][:], adj_in[par][:], 0.0, MASKED, ALU.is_equal,
                                  ALU.mult).then_inc(mask_made, 1)

            def group(g, par, k):
                first = isinstance(g, int) and g == 0
                nxt = 1 - par
                for s in range(SLOTS):
                    if first and s == 0:
                        low_part_bank(g, 0, par)
                    if has_next(g) or s == 0:
                        masked_max(g, s, par)
                    if not has_next(g) and s < SLOTS - 1:
                        masked_max(g, s + 1, par)
                    filled = s if first else s - 1
                    bank_to_split = filled in SPLIT_RANK and has_next(g) and not (first and s == 0)
                    if bank_to_split and s != 1:
                        low_part_bank(g, filled, par)
                    if s >= 2:
                        head_norm(g, s - 2)
                    elif not first:
                        head_norm(g - 1, SLOTS - 2 + s)
                    if bank_to_split and s == 1:
                        low_part_bank(g, filled, par)
                    if s > 0:
                        low_part_probs(g, s - 1)
                    elif not first:
                        low_part_probs(g - 1, SLOTS - 1)
                    if s == 2 and not first or s == 6:
                        low_part_attn(aT_no(g, s - 1))
                    if s == 0 and not first:
                        y_and_moments(g - 1, 0, (g - 1, 7), nxt)
                    if s == 5 and not first:
                        y_and_moments(g - 1, 1, (g, 4), nxt)
                    if s == 4 and first:
                        dve.wait_ge(b_out_mm, 1)
                        dve.wait_ge(bo_loaded, 16)
                        dve.tensor_tensor(b_out[:], b_out_ps[:], b_out[:], ALU.add).then_inc(b_out_made, 1)
                    if s == 4 and has_next(g):
                        make_mask(g + 1, nxt, k + par)

            for i in range(2):
                dve.memset(v_parts[i][:, :, :, V_ONE:VC], UP).then_inc(ones_made, 1)
            for h in range(2):
                low_part_x(dve, 0, h, 0)
            for i, n in enumerate("qkvo"):
                if n == "o":
                    make_mask(0, 0, 0)
                for c in range(KC):
                    dve.wait_ge(w_hi_made, i * KC + c + 1)
                    dve.scalar_tensor_tensor(out=w_lo[n][:, c], in0=w_raw[n][:, c], scalar=1.0 if n == "o" else UP,
                                             in1=w_hi[n][:, c].bitcast(F32), op0=ALU.mult,
                                             op1=ALU.subtract).then_inc(w_lo_made, 1)
                if n == "q":
                    dve.wait_ge(bias_loaded, 16)
                    dve.tensor_scalar(b_qk_up[:], b_raw[:, 0:2], UP, None, ALU.mult).then_inc(bias_made, 1)
                    dve.tensor_copy(b_v_wide[:],
                                    b_raw[:, 2].unsqueeze(2).to_broadcast([P, KC, P])).then_inc(bias_made, 1)
                if n == "k":
                    dve.wait_ge(bias_made, 1)
                    low_part_bank(-1, 0, 1)
                    low_part_bank(-1, 1, 1)
                if n == "v":
                    low_part_bank(-1, 2, 1)
                    low_part_bank(-1, 3, 1)
                    for h in range(2):
                        low_part_x(dve, 1, h, 1)
                    low_part_bank(-1, 5, 1)
                    low_part_bank(-1, 6, 1)
            all_groups(dve, group)
            head_norm(LAST, SLOTS - 2)
            low_part_probs(LAST, SLOTS - 1)
            head_norm(LAST, SLOTS - 1)
            low_part_attn(aT_no(LAST, 9))
            y_and_moments(LAST, 0, (LAST, 7), LAST % 2)
            y_and_moments(LAST, 1, (LAST, 8), LAST % 2)

        @block.tensor
        def _(pe):
            def mm(dst, lhsT, rhs, first, last):
                return pe.matmul(dst, lhsT, rhs, start=first, stop=last)

            def transpose_attn(count, b, last_unit):
                pe.wait_ge(attn_done, last_unit + 1)
                if isinstance(count, int) and count == 0:
                    pe.wait_ge(b_out_made, 1)
                else:
                    pe.wait_ge(aT_out, count)
                for c in range(KC):
                    ins = pe.transpose(aT_ps[:, c], attn[b][:, c * P:(c + 1) * P], ident[:])
                ins.then_inc(aT_done, 1)

            def weight_made(kind, ki):
                pe.wait_ge(w_lo_made, "qkvo".index(kind) * KC + ki + 1)

            def qk_bank(kind, half, dst, par, fresh):
                for c in range(2):
                    cols = slice((2 * half + c) * P, (2 * half + c + 1) * P)
                    o = dst[:, c * TOK:(c + 1) * TOK]
                    for ki in range(KC):
                        if fresh and c == 0:
                            weight_made(kind, ki)
                        hi, lo = w_hi[kind][:, ki, cols], w_lo[kind][:, ki, cols]
                        mm(o, hi, xT_hi[par][:, ki], ki == 0, False)
                        mm(o, hi, xT_lo[par][:, ki], False, False)
                        ins = mm(o, lo, xT_hi[par][:, ki], False, ki == KC - 1)
                return ins

            def row_bank(dst, a_hi, a_lo, n, cols, fresh):
                for ki in range(KC):
                    if fresh:
                        weight_made(n, ki)
                    mm(dst[:], a_hi[:, ki, cols], w_hi[n][:, ki], ki == 0, False)
                    mm(dst[:], a_hi[:, ki, cols], w_lo[n][:, ki], False, False)
                    ins = mm(dst[:], a_lo[:, ki, cols], w_hi[n][:, ki], False, ki == KC - 1)
                return ins

            def bank_before(g, s):
                if s is None or isinstance(g, int) and g == -1 and s == 0:
                    return g, None
                g, s = (g, s - 1) if s > 0 else (g - 1, SLOTS - 1)
                if isinstance(g, int):
                    none = {-1: (4, 7), 0: (4,), LAST: (0, 1, 2, 3, 5, 6)}.get(g, ())
                    if s in none:
                        return bank_before(g, s)
                return g, s

            def bank(g, s, par, fresh=False):
                kind, i = TASKS[s]
                dst = proj_ps[bank_of(g, s)]
                before, slot = bank_before(*bank_before(g, s))
                if slot is None:
                    pass
                elif TASKS[slot][0] == Y:
                    pe.wait_ge(y_summed, batch(before - 1 if slot == 4 else before, TASKS[slot][1]) + 1)
                else:
                    pe.wait_ge(split_out, split_no(before, slot) + 1)
                if kind in (Q, K):
                    ins = qk_bank(kind, i, dst, par, fresh)
                elif kind == V:
                    ins = row_bank(dst, xT_hi[par], xT_lo[par], "v", slice(i * S, (i + 1) * S), fresh)
                else:
                    ins = row_bank(dst, aT_hi, aT_lo, "o", slice(0, S), fresh)
                ins.then_inc(bank_done, 1)

            def scores(g, s, par, k):
                u = unit(g, s)
                b, c = s // KC, s % KC
                if s == 0:
                    pe.wait_ge(stacked["q"][par], 32 * dma_round(g, k))
                    pe.wait_ge(stacked["k"][par], 16 * dma_round(g, k))
                wait(pe, max_done, u - 1)
                toks = slice(b * S, (b + 1) * S)
                for j in range(HC):
                    h = HC * c + j
                    ins = mm(score_ps[s % 2][:, j], stacks["q"][par][:, h, toks], stacks["k"][par][:, h, toks],
                             True, True)
                ins.then_inc(score_done, 1)

            def transpose_probs(g, s):
                u = unit(g, s)
                pe.wait_ge(exp_done, u + 1)
                wait(pe, pT_out, u - 1)
                for j in range(HC):
                    ins = pe.transpose(pT_ps[s % 2][:, j], probs[s % 2][:, j], ident[:])
                ins.then_inc(pT_done, 1)

            def attend(g, s, par):
                u = unit(g, s)
                b, c = s // KC, s % KC
                pe.wait_ge(pT_out, u + 1)
                wait(pe, norm_done, u)
                if c == 0:
                    pe.wait_ge(split_out, split_no(g - 1, 5 + b) + 1)
                for j in range(HC):
                    h = HC * c + j
                    mm(av_view[:, j, 0:VC], pT_hi[s % 2][:, j], v_parts[par][:, b, h, 0:VC], True, False)
                    ins = mm(av_view[:, j, V_HI:VC], pT_lo[s % 2][:, j], v_parts[par][:, b, h, V_HI:VC], False, True)
                ins.then_inc(av_done, 1)

            def output_bank(g, s, fresh=False):
                pe.wait_ge(aT_out, aT_no(g, {4: 1, 7: 5, 8: 9}[s]) + 1)
                bank(g, s, None, fresh)

            def next_group_bank(g, s, nxt):
                if s == 0:
                    pe.wait_ge(x_lo_done, x_half_no(g + 2, 0))
                bank(g, s, nxt)

            def first_group(g, par, k):
                nxt = 1 - par
                next_group_bank(g, 0, nxt)
                scores(g, 0, par, k)
                scores(g, 1, par, k)
                next_group_bank(g, 1, nxt)
                pe.wait_ge(ones_made, 2)
                for s in range(1, SLOTS):
                    transpose_probs(g, s - 1)
                    if s == 3:
                        pe.wait_ge(w_loaded["o"][0], 16)
                        pe.wait_ge(bias_made, 2)
                        for ki in range(KC):
                            ins = mm(b_out_ps[:], b_v_wide[:, ki], w_raw["o"][:, ki], ki == 0, ki == KC - 1)
                        ins.then_inc(b_out_mm, 1)
                    elif s < 6:
                        next_group_bank(g, s + 1, nxt)
                    elif s == 7:
                        output_bank(g, 7, fresh=True)
                    if s == 5:
                        transpose_attn(aT_no(g, 5), 0, unit(g, 3))
                    if s < SLOTS - 1:
                        scores(g, s + 1, par, k)
                    else:
                        scores(g + 1, 0, nxt, k + par)
                    attend(g, s - 1, par)

            def group(g, par, k):
                nxt = 1 - par
                for s in range(SLOTS):
                    if s > 0:
                        transpose_probs(g, s - 1)
                    else:
                        transpose_probs(g - 1, SLOTS - 1)
                    if TASKS[s][0] == Y:
                        output_bank(g, s)
                    else:
                        next_group_bank(g, s, nxt)
                    if s == 1:
                        transpose_attn(aT_no(g, 1), 1, unit(g - 1, SLOTS - 1))
                    if s == 5:
                        transpose_attn(aT_no(g, 5), 0, unit(g, 3))
                    if s < SLOTS - 1:
                        scores(g, s + 1, par, k)
                    else:
                        scores(g + 1, 0, nxt, k + par)
                    if s > 0:
                        attend(g, s - 1, par)
                    else:
                        attend(g - 1, SLOTS - 1, nxt)

            def last_group(g, par, k):
                for s in range(SLOTS):
                    if s < SLOTS - 1:
                        scores(g, s + 1, par, k)
                    if s > 0:
                        transpose_probs(g, s - 1)
                    else:
                        transpose_probs(g - 1, SLOTS - 1)
                    if s > 1:
                        attend(g, s - 2, par)
                    elif s == 1:
                        attend(g - 1, SLOTS - 1, 1 - par)
                    if s == 2:
                        transpose_attn(aT_no(g, 1), 1, unit(g - 1, SLOTS - 1))
                    if s == 6:
                        transpose_attn(aT_no(g, 5), 0, unit(g, 3))
                    if s == 4:
                        output_bank(g, 4)
                transpose_probs(g, SLOTS - 1)
                attend(g, SLOTS - 2, par)
                attend(g, SLOTS - 1, par)
                output_bank(g, 7)
                transpose_attn(aT_no(g, 9), 1, unit(g, SLOTS - 1))
                output_bank(g, 8)

            pe.wait_ge(x_lo_done, 2)
            for s in SPLIT_RANK:
                bank(-1, s, 0, fresh=TASKS[s][1] == 0)
            pe.wait_ge(const_made, 2)
            all_groups(pe, group, first_group, last_group)


def layouts(x, adj, weights, biases, bo):
    import numpy as np

    B, S, D = x.shape
    KC = D // P
    return {
        "x_rows": x.reshape(B // GB, GB, S, D).transpose(0, 2, 1, 3),
        "x_cols": x.reshape(B // GB, GB * S, KC, P).transpose(0, 3, 2, 1),
        "adj": adj.reshape(B // GB, GB, S, S).transpose(0, 2, 1, 3),
        "weights": np.stack([w.reshape(KC, P, D).transpose(1, 0, 2) for w in weights]),
        "biases": np.stack([b.reshape(KC, P).T for b in biases], axis=1),
        "bo": bo,
    }


def kernel(x, adj, L0_gnn_Wq, L0_gnn_bq, L0_gnn_Wk, L0_gnn_bk, L0_gnn_Wv, L0_gnn_bv, L0_gnn_Wo, L0_gnn_bo):
    import numpy as np
    import concourse.bacc as bacc
    from concourse.bass_utils import run_bass_kernel_spmd

    nc = bacc.Bacc("TRN2", target_bir_lowering=False, num_devices=1)
    x, adj, bo = np.asarray(x), np.asarray(adj), np.asarray(L0_gnn_bo)
    weights = [np.asarray(w) for w in (L0_gnn_Wq, L0_gnn_Wk, L0_gnn_Wv, L0_gnn_Wo)]
    biases = [np.asarray(b) for b in (L0_gnn_bq, L0_gnn_bk, L0_gnn_bv)]
    arrays = {n: np.ascontiguousarray(a) for n, a in layouts(x, adj, weights, biases, bo).items()}
    args = [nc.dram_tensor(n, a.shape, mybir.dt.from_np(a.dtype), kind="ExternalInput").ap()
            for n, a in arrays.items()]
    out = nc.dram_tensor("out", x.shape, F32, kind="ExternalOutput").ap()
    build_program(nc, *args, out)
    return run_bass_kernel_spmd(nc, [arrays], core_ids=[0]).results[0]["out"]
```
